# Optimizing a Trainium2 kernel written in Bass

```python
import numpy as np
import jax
import jax.numpy as jnp

def _softmax(x, axis=-1):
    return jax.nn.softmax(x, axis=axis)

def _gelu(x):
    return jax.nn.gelu(x, approximate=True)

def _silu(x):
    return jax.nn.silu(x)

def _sigmoid(x):
    return jax.nn.sigmoid(x)

def _layernorm(x, axis=-1, eps=1e-05):
    m = jnp.mean(x, axis=axis, keepdims=True)
    v = jnp.var(x, axis=axis, keepdims=True)
    return (x - m) / jnp.sqrt(v + eps)

def _scatter_add(tgt, idx, src, axis=0):
    return tgt.at[idx].add(src)

def _segment_sum(src, seg, n):
    return jax.ops.segment_sum(src, seg, n)
kernel_name = 'mk_xattn_seq_d4_seqx_r8_1eadba'

def setup_inputs(seed: int=0):
    np.random.seed(seed)
    _w = jnp.asarray

    def _rec_inputs():
        import jax
        import jax.numpy as jnp
        _rk = jax.random.key(seed)
        x = 7.22e-05 + 1 * jax.random.normal(jax.random.fold_in(_rk, 1), (64, 128, 128), jnp.float32)
        _lenS = 128 - jax.random.randint(jax.random.fold_in(_rk, 7), (64,), 0, max(1, 128 // 4) + 1, jnp.int32)
        _lenS2 = 77 - jax.random.randint(jax.random.fold_in(_rk, 8), (64,), 0, max(1, 77 // 4) + 1, jnp.int32)
        _ctx_2048P = jax.random.normal(jax.random.fold_in(_rk, 11), (64, 16, 256), jnp.float32)
        _ctx_2048c = jax.random.dirichlet(jax.random.fold_in(_rk, 511), 0.3 * jnp.ones((16,), jnp.float32), (64, 77))
        _ctx_2048t = jnp.einsum('bsk,bkd->bsd', _ctx_2048c, _ctx_2048P)
        _ctx_2048t = _ctx_2048t * jax.lax.rsqrt(jnp.mean(jnp.square(_ctx_2048t)) + 1e-12) * 0.953939
        ctx_2048 = -1.39393e-06 + 0.999914 * (_ctx_2048t + 0.3 * jax.random.normal(jax.random.fold_in(_rk, 611), (64, 77, 256), jnp.float32))
        _validS = jnp.arange(128)[None, :] < _lenS[:, None]
        _validS2 = jnp.arange(77)[None, :] < _lenS2[:, None]
        _causal = jnp.tril(jnp.ones((128, 128), dtype=bool))
        mask_S_fk1 = jnp.where(_validS[0], 1.0, 0.0).astype(jnp.float32)
        mask_S_fk0 = jnp.where(_validS[0], 0.0, 1.0).astype(jnp.float32)
        return (x, ctx_2048, mask_S_fk1, mask_S_fk0)
    x, ctx_2048, mask_S_fk1, mask_S_fk0 = _rec_inputs()

    def _L0_xattn_setup():
        import jax, jax.numpy as jnp
        import numpy as np
        D_MODEL = 128
        N_HEADS = 16
        N_KV_HEADS = 4
        HEAD_DIM = D_MODEL // N_HEADS
        SPEAKER_DIM = 256
        EPS = 1e-05

        def rmsnorm(x, w, eps=EPS):
            xf = x.astype(jnp.float32)
            inv = jax.lax.rsqrt(jnp.mean(xf * xf, axis=-1, keepdims=True) + eps)
            return (xf * inv).astype(x.dtype) * w
        key = jax.random.key(seed)
        ks = jax.random.split(key, 7)
        B, T, S = (4, 256, 64)
        x = jax.random.normal(ks[0], (B, T, D_MODEL), dtype=jnp.float32)
        cond = jax.random.normal(ks[1], (B, S, SPEAKER_DIM), dtype=jnp.float32)
        sq = 0.02
        wq = jax.random.normal(ks[2], (D_MODEL, N_HEADS * HEAD_DIM), dtype=jnp.float32) * sq
        wk = jax.random.normal(ks[3], (SPEAKER_DIM, N_KV_HEADS * HEAD_DIM), dtype=jnp.float32) * sq
        wv = jax.random.normal(ks[4], (SPEAKER_DIM, N_KV_HEADS * HEAD_DIM), dtype=jnp.float32) * sq
        wo = jax.random.normal(ks[5], (N_HEADS * HEAD_DIM, D_MODEL), dtype=jnp.float32) * sq
        norm_w = jnp.ones((D_MODEL,), dtype=jnp.float32)
        return {'x': x, 'cond': cond, 'wq': wq, 'wk': wk, 'wv': wv, 'wo': wo, 'norm_w': norm_w}
    _L0_xattn_all = _L0_xattn_setup()
    _L0_xattn_in = {k: v for k, v in _L0_xattn_all.items() if k in ('wq', 'wk', 'wv', 'wo', 'norm_w')}
    del _L0_xattn_all

    def _L1_xattn_setup():
        import jax, jax.numpy as jnp
        import numpy as np
        HEADS = 16
        HEAD_DIM = 64
        SUPPRESS = 20.0
        key = jax.random.key(seed)
        ks = jax.random.split(key, 8)
        B, HW, C, T, CT = (8, 512, 128, 77, 256)
        inner = HEADS * HEAD_DIM
        scale = 0.02
        return {'hidden_states': jax.random.normal(ks[0], (B, HW, C), jnp.float32), 'encoder_hidden_states': jax.random.normal(ks[1], (B, T, CT), jnp.float32), 'mask_A': (jax.random.uniform(ks[2], (HW,)) > 0.5).astype(jnp.float32), 'mask_B': (jax.random.uniform(ks[3], (HW,)) > 0.5).astype(jnp.float32), 'Wq': jax.random.normal(ks[4], (C, inner), jnp.float32) * scale, 'Wk': jax.random.normal(ks[5], (CT, inner), jnp.float32) * scale, 'Wv': jax.random.normal(ks[6], (CT, inner), jnp.float32) * scale, 'Wo': jax.random.normal(ks[7], (inner, C), jnp.float32) * scale, 'bo': jnp.zeros((C,), jnp.float32), 'token_indices_A': jnp.array([2, 3], dtype=jnp.int64), 'token_indices_B': jnp.array([5, 6], dtype=jnp.int64)}
    _L1_xattn_all = _L1_xattn_setup()
    _L1_xattn_in = {k: v for k, v in _L1_xattn_all.items() if k in ('Wq', 'Wk', 'Wv', 'Wo', 'bo', 'token_indices_A', 'token_indices_B')}
    del _L1_xattn_all

    def _L2_xattn_setup():
        import jax, jax.numpy as jnp
        import numpy as np
        D_MODEL = 128
        N_HEADS = 16
        N_KV_HEADS = 4
        HEAD_DIM = D_MODEL // N_HEADS
        SPEAKER_DIM = 256
        EPS = 1e-05

        def rmsnorm(x, w, eps=EPS):
            xf = x.astype(jnp.float32)
            inv = jax.lax.rsqrt(jnp.mean(xf * xf, axis=-1, keepdims=True) + eps)
            return (xf * inv).astype(x.dtype) * w
        key = jax.random.key(seed)
        ks = jax.random.split(key, 7)
        B, T, S = (4, 256, 64)
        x = jax.random.normal(ks[0], (B, T, D_MODEL), dtype=jnp.float32)
        cond = jax.random.normal(ks[1], (B, S, SPEAKER_DIM), dtype=jnp.float32)
        sq = 0.02
        wq = jax.random.normal(ks[2], (D_MODEL, N_HEADS * HEAD_DIM), dtype=jnp.float32) * sq
        wk = jax.random.normal(ks[3], (SPEAKER_DIM, N_KV_HEADS * HEAD_DIM), dtype=jnp.float32) * sq
        wv = jax.random.normal(ks[4], (SPEAKER_DIM, N_KV_HEADS * HEAD_DIM), dtype=jnp.float32) * sq
        wo = jax.random.normal(ks[5], (N_HEADS * HEAD_DIM, D_MODEL), dtype=jnp.float32) * sq
        norm_w = jnp.ones((D_MODEL,), dtype=jnp.float32)
        return {'x': x, 'cond': cond, 'wq': wq, 'wk': wk, 'wv': wv, 'wo': wo, 'norm_w': norm_w}
    _L2_xattn_all = _L2_xattn_setup()
    _L2_xattn_in = {k: v for k, v in _L2_xattn_all.items() if k in ('wq', 'wk', 'wv', 'wo', 'norm_w')}
    del _L2_xattn_all

    def _L3_xattn_setup():
        import jax, jax.numpy as jnp
        import numpy as np
        HEADS = 16
        HEAD_DIM = 64
        SUPPRESS = 20.0
        key = jax.random.key(seed)
        ks = jax.random.split(key, 8)
        B, HW, C, T, CT = (8, 512, 128, 77, 256)
        inner = HEADS * HEAD_DIM
        scale = 0.02
        return {'hidden_states': jax.random.normal(ks[0], (B, HW, C), jnp.float32), 'encoder_hidden_states': jax.random.normal(ks[1], (B, T, CT), jnp.float32), 'mask_A': (jax.random.uniform(ks[2], (HW,)) > 0.5).astype(jnp.float32), 'mask_B': (jax.random.uniform(ks[3], (HW,)) > 0.5).astype(jnp.float32), 'Wq': jax.random.normal(ks[4], (C, inner), jnp.float32) * scale, 'Wk': jax.random.normal(ks[5], (CT, inner), jnp.float32) * scale, 'Wv': jax.random.normal(ks[6], (CT, inner), jnp.float32) * scale, 'Wo': jax.random.normal(ks[7], (inner, C), jnp.float32) * scale, 'bo': jnp.zeros((C,), jnp.float32), 'token_indices_A': jnp.array([2, 3], dtype=jnp.int64), 'token_indices_B': jnp.array([5, 6], dtype=jnp.int64)}
    _L3_xattn_all = _L3_xattn_setup()
    _L3_xattn_in = {k: v for k, v in _L3_xattn_all.items() if k in ('Wq', 'Wk', 'Wv', 'Wo', 'bo', 'token_indices_A', 'token_indices_B')}
    del _L3_xattn_all
    return {'x': x, 'ctx_2048': ctx_2048, 'mask_S_fk1': mask_S_fk1, 'mask_S_fk0': mask_S_fk0, 'L0_xattn_wq': _L0_xattn_in['wq'], 'L0_xattn_wk': _L0_xattn_in['wk'], 'L0_xattn_wv': _L0_xattn_in['wv'], 'L0_xattn_wo': _L0_xattn_in['wo'], 'L0_xattn_norm_w': _L0_xattn_in['norm_w'], 'L1_xattn_Wq': _L1_xattn_in['Wq'], 'L1_xattn_Wk': _L1_xattn_in['Wk'], 'L1_xattn_Wv': _L1_xattn_in['Wv'], 'L1_xattn_Wo': _L1_xattn_in['Wo'], 'L1_xattn_bo': _L1_xattn_in['bo'], 'L1_xattn_token_indices_A': _L1_xattn_in['token_indices_A'], 'L1_xattn_token_indices_B': _L1_xattn_in['token_indices_B'], 'L2_xattn_wq': _L2_xattn_in['wq'], 'L2_xattn_wk': _L2_xattn_in['wk'], 'L2_xattn_wv': _L2_xattn_in['wv'], 'L2_xattn_wo': _L2_xattn_in['wo'], 'L2_xattn_norm_w': _L2_xattn_in['norm_w'], 'L3_xattn_Wq': _L3_xattn_in['Wq'], 'L3_xattn_Wk': _L3_xattn_in['Wk'], 'L3_xattn_Wv': _L3_xattn_in['Wv'], 'L3_xattn_Wo': _L3_xattn_in['Wo'], 'L3_xattn_bo': _L3_xattn_in['bo'], 'L3_xattn_token_indices_A': _L3_xattn_in['token_indices_A'], 'L3_xattn_token_indices_B': _L3_xattn_in['token_indices_B']}

def reference(x, ctx_2048, mask_S_fk1, mask_S_fk0, L0_xattn_wq, L0_xattn_wk, L0_xattn_wv, L0_xattn_wo, L0_xattn_norm_w, L1_xattn_Wq, L1_xattn_Wk, L1_xattn_Wv, L1_xattn_Wo, L1_xattn_bo, L1_xattn_token_indices_A, L1_xattn_token_indices_B, L2_xattn_wq, L2_xattn_wk, L2_xattn_wv, L2_xattn_wo, L2_xattn_norm_w, L3_xattn_Wq, L3_xattn_Wk, L3_xattn_Wv, L3_xattn_Wo, L3_xattn_bo, L3_xattn_token_indices_A, L3_xattn_token_indices_B):
    import jax
    import jax.numpy as jnp

    def _L0_xattn_ref(x, cond, wq, wk, wv, wo, norm_w):
        import jax, jax.numpy as jnp
        import numpy as np
        D_MODEL = 128
        N_HEADS = 16
        N_KV_HEADS = 4
        HEAD_DIM = D_MODEL // N_HEADS
        SPEAKER_DIM = 256
        EPS = 1e-05

        def rmsnorm(x, w, eps=EPS):
            xf = x.astype(jnp.float32)
            inv = jax.lax.rsqrt(jnp.mean(xf * xf, axis=-1, keepdims=True) + eps)
            return (xf * inv).astype(x.dtype) * w
        B, T, _ = x.shape
        S = cond.shape[1]
        n_rep = N_HEADS // N_KV_HEADS
        residual = x
        xn = rmsnorm(x, norm_w)
        q = (xn @ wq).reshape(B, T, N_HEADS, HEAD_DIM)
        k = (cond @ wk).reshape(B, S, N_KV_HEADS, HEAD_DIM)
        v = (cond @ wv).reshape(B, S, N_KV_HEADS, HEAD_DIM)
        qg = q.reshape(B, T, N_KV_HEADS, n_rep, HEAD_DIM)
        scale = 1.0 / np.sqrt(HEAD_DIM).astype(np.float32)
        scores = jnp.einsum('btgrd,bsgd->bgrts', qg, k) * scale
        attn = jax.nn.softmax(scores.astype(jnp.float32), axis=-1).astype(q.dtype)
        out = jnp.einsum('bgrts,bsgd->btgrd', attn, v).reshape(B, T, N_HEADS * HEAD_DIM)
        return residual + out @ wo

    def _L1_xattn_ref(hidden_states, encoder_hidden_states, mask_A, mask_B, Wq, Wk, Wv, Wo, bo, token_indices_A, token_indices_B):
        import jax, jax.numpy as jnp
        import numpy as np
        HEADS = 16
        HEAD_DIM = 64
        SUPPRESS = 20.0
        B, HW, C = hidden_states.shape
        T = encoder_hidden_states.shape[1]
        residual = hidden_states
        q = hidden_states @ Wq
        k = encoder_hidden_states @ Wk
        v = encoder_hidden_states @ Wv
        q = q.reshape(B, HW, HEADS, HEAD_DIM).transpose(0, 2, 1, 3)
        k = k.reshape(B, T, HEADS, HEAD_DIM).transpose(0, 2, 1, 3)
        v = v.reshape(B, T, HEADS, HEAD_DIM).transpose(0, 2, 1, 3)
        scale = HEAD_DIM ** (-0.5)
        logits = jnp.einsum('bhqd,bhkd->bhqk', q, k) * scale
        suppress_A_in = 1.0 - mask_A
        suppress_B_in = 1.0 - mask_B
        col_bias = jnp.zeros((HW, T), logits.dtype)
        col_bias = col_bias.at[:, token_indices_A].set((-SUPPRESS * suppress_A_in)[:, None])
        col_bias = col_bias.at[:, token_indices_B].set((-SUPPRESS * suppress_B_in)[:, None])
        logits = logits + col_bias[None, None, :, :]
        probs = jax.nn.softmax(logits, axis=-1)
        out = jnp.einsum('bhqk,bhkd->bhqd', probs, v)
        out = out.transpose(0, 2, 1, 3).reshape(B, HW, HEADS * HEAD_DIM)
        out = out @ Wo + bo
        out = out + residual
        return out

    def _L2_xattn_ref(x, cond, wq, wk, wv, wo, norm_w):
        import jax, jax.numpy as jnp
        import numpy as np
        D_MODEL = 128
        N_HEADS = 16
        N_KV_HEADS = 4
        HEAD_DIM = D_MODEL // N_HEADS
        SPEAKER_DIM = 256
        EPS = 1e-05

        def rmsnorm(x, w, eps=EPS):
            xf = x.astype(jnp.float32)
            inv = jax.lax.rsqrt(jnp.mean(xf * xf, axis=-1, keepdims=True) + eps)
            return (xf * inv).astype(x.dtype) * w
        B, T, _ = x.shape
        S = cond.shape[1]
        n_rep = N_HEADS // N_KV_HEADS
        residual = x
        xn = rmsnorm(x, norm_w)
        q = (xn @ wq).reshape(B, T, N_HEADS, HEAD_DIM)
        k = (cond @ wk).reshape(B, S, N_KV_HEADS, HEAD_DIM)
        v = (cond @ wv).reshape(B, S, N_KV_HEADS, HEAD_DIM)
        qg = q.reshape(B, T, N_KV_HEADS, n_rep, HEAD_DIM)
        scale = 1.0 / np.sqrt(HEAD_DIM).astype(np.float32)
        scores = jnp.einsum('btgrd,bsgd->bgrts', qg, k) * scale
        attn = jax.nn.softmax(scores.astype(jnp.float32), axis=-1).astype(q.dtype)
        out = jnp.einsum('bgrts,bsgd->btgrd', attn, v).reshape(B, T, N_HEADS * HEAD_DIM)
        return residual + out @ wo

    def _L3_xattn_ref(hidden_states, encoder_hidden_states, mask_A, mask_B, Wq, Wk, Wv, Wo, bo, token_indices_A, token_indices_B):
        import jax, jax.numpy as jnp
        import numpy as np
        HEADS = 16
        HEAD_DIM = 64
        SUPPRESS = 20.0
        B, HW, C = hidden_states.shape
        T = encoder_hidden_states.shape[1]
        residual = hidden_states
        q = hidden_states @ Wq
        k = encoder_hidden_states @ Wk
        v = encoder_hidden_states @ Wv
        q = q.reshape(B, HW, HEADS, HEAD_DIM).transpose(0, 2, 1, 3)
        k = k.reshape(B, T, HEADS, HEAD_DIM).transpose(0, 2, 1, 3)
        v = v.reshape(B, T, HEADS, HEAD_DIM).transpose(0, 2, 1, 3)
        scale = HEAD_DIM ** (-0.5)
        logits = jnp.einsum('bhqd,bhkd->bhqk', q, k) * scale
        suppress_A_in = 1.0 - mask_A
        suppress_B_in = 1.0 - mask_B
        col_bias = jnp.zeros((HW, T), logits.dtype)
        col_bias = col_bias.at[:, token_indices_A].set((-SUPPRESS * suppress_A_in)[:, None])
        col_bias = col_bias.at[:, token_indices_B].set((-SUPPRESS * suppress_B_in)[:, None])
        logits = logits + col_bias[None, None, :, :]
        probs = jax.nn.softmax(logits, axis=-1)
        out = jnp.einsum('bhqk,bhkd->bhqd', probs, v)
        out = out.transpose(0, 2, 1, 3).reshape(B, HW, HEADS * HEAD_DIM)
        out = out @ Wo + bo
        out = out + residual
        return out
    x = _L0_xattn_ref(x, ctx_2048, L0_xattn_wq, L0_xattn_wk, L0_xattn_wv, L0_xattn_wo, L0_xattn_norm_w)
    x = _L1_xattn_ref(x, ctx_2048, mask_S_fk1, mask_S_fk0, L1_xattn_Wq, L1_xattn_Wk, L1_xattn_Wv, L1_xattn_Wo, L1_xattn_bo, L1_xattn_token_indices_A, L1_xattn_token_indices_B)
    x = _L2_xattn_ref(x, ctx_2048, L2_xattn_wq, L2_xattn_wk, L2_xattn_wv, L2_xattn_wo, L2_xattn_norm_w)
    x = _L3_xattn_ref(x, ctx_2048, mask_S_fk1, mask_S_fk0, L3_xattn_Wq, L3_xattn_Wk, L3_xattn_Wv, L3_xattn_Wo, L3_xattn_bo, L3_xattn_token_indices_A, L3_xattn_token_indices_B)
    return x

_drawn_inputs = setup_inputs


def setup_inputs(seed=0):
    import zlib

    import numpy as np

    out = dict(_drawn_inputs(seed))
    spreads = {'L0_xattn_norm_w': (1.0, 0.6),
     'L1_xattn_bo': (0.0, 0.1),
     'L2_xattn_norm_w': (1.0, 0.6),
     'L3_xattn_bo': (0.0, 0.1)}
    factors = {'mask_S_fk1': 8.0,
     'mask_S_fk0': 8.0,
     'L0_xattn_wq': 8.0,
     'L0_xattn_wk': 8.0,
     'L1_xattn_Wq': 8.0,
     'L1_xattn_Wk': 8.0,
     'L2_xattn_wq': 8.0,
     'L2_xattn_wk': 8.0,
     'L3_xattn_Wq': 8.0,
     'L3_xattn_Wk': 8.0}
    for name, (base, spread) in spreads.items():
        noise = np.random.default_rng([zlib.crc32(name.encode()), seed]).standard_normal(out[name].shape)
        drawn = base * np.exp(spread * noise) if base else spread * noise
        out[name] = jnp.asarray(drawn.astype(out[name].dtype))
    for name, factor in factors.items():
        out[name] = (out[name] * factor).astype(out[name].dtype)
    return out
```

```python
from contextlib import ExitStack

import numpy as np

import concourse.bass as bass
from concourse import mybir

ALU = mybir.AluOpType
ACT = mybir.ActivationFunctionType
AX_X = mybir.AxisListType.X
F32 = mybir.dt.float32
F16 = mybir.dt.float16
BF16 = mybir.dt.bfloat16
I32 = mybir.dt.int32

P = 128
H = 16
EPS = 1e-5
SUPPRESS = 20.0
STREAMS = 2
LAYERS = 4
SLOTS = STREAMS * LAYERS
HI, LO = 0, 1


def build(nc, x_d, ctx_d, mask_a_d, mask_b_d, gqa_w, mha_w, out_d):
    B, T, D = x_d.shape
    S, C = ctx_d.shape[1:]
    KC = C // P
    GD = D // H
    KVG = gqa_w[0]["wk"].shape[1] // GD
    R = H // KVG
    INNER = mha_w[0]["Wq"].shape[1]
    MD = INNER // H
    NOC = INNER // P
    HPC = P // MD
    HS = H * S
    HS_PAD = (H - 1) * S + P
    BANK = 512
    NIT = B // STREAMS
    assert T == P and D == P and GD * R * 4 == P and HS <= 3 * BANK

    W_GQA = 16.0
    W_M = 16.0
    W_V = 64.0
    W_P = 4096.0
    MHA_SCALE = float(MD) ** -0.5 / W_M
    Y_SCALE = 1.0 / (W_V * W_V)
    SS_MUL = GD * W_GQA ** 4 / D
    SS_ADD = GD * W_GQA ** 4 * EPS

    def layer(j):
        return (j % SLOTS) // STREAMS

    def is_gqa(j):
        return layer(j) % 2 == 0

    HEADS_G = BANK // S
    G_CHUNKS = [(h, min(H, h + HEADS_G)) for h in range(0, H, HEADS_G)]
    V_CHUNKS = [(n, n + BANK) for n in range(0, INNER, BANK)]
    HEADS_O = 6
    TURN = 4
    NTURN = H // TURN
    NOT = NOC // TURN

    gqa_only, mha_only = (1, 0, 1, 0), (0, 1, 0, 1)
    first_only, last_only, each = (1, 0, 0, 0), (0, 0, 0, 1), (1, 1, 1, 1)
    n_ctx = (2, len(G_CHUNKS) + len(V_CHUNKS)) * 2
    n_flip = (NTURN + 1, NTURN + NOT) * 2
    n_o = (1, 2, 1, 2)
    PER_ITEM = {
        "q_raw": gqa_only, "q_hi": gqa_only, "q_lo": gqa_only, "kb": gqa_only,
        "ms": gqa_only, "rstd": gqa_only, "sq": gqa_only, "xb": mha_only,
        "s_raw": each, "s_max": each, "s_sub": each, "p_exp": each,
        "ctx_raw": n_ctx, "ctx_hi": n_ctx, "ctx_lo": n_ctx,
        "flip_raw": n_flip, "flip_hi": n_flip, "flip_lo": n_flip,
        "o_raw": n_o, "o_rcp": n_o, "o_norm": n_o,
        "y_raw": each, "x_f32": each, "x_hi": each, "x_lo": each,
        "x_in": first_only, "ct_raw": first_only, "ct_hi": first_only, "ct_lo": first_only,
        "xr_raw": last_only, "xr": last_only, "out": last_only,
    }

    def at(name, it, j, k):
        per = [PER_ITEM[name][layer(n)] for n in range(SLOTS)]
        return (it + j // SLOTS) * sum(per) + sum(per[:j % SLOTS]) + k

    def m_place(h):
        return h % HPC * NOC + h // HPC

    def exists(it, j):
        return not isinstance(it, int) or 0 <= it * SLOTS + j < NIT * SLOTS

    def buffer_of(name, j, k):
        return at(name, 0, j, k) % 2

    with ExitStack() as ctx:
        def sb(name, shape, dt):
            return ctx.enter_context(nc.sbuf_tensor(name, shape, dt))

        def ps(name, shape):
            return ctx.enter_context(nc.psum_tensor(name, shape, F32))

        def sem(name):
            return ctx.enter_context(nc.semaphore(name))

        wq_r = [sb(f"wq_r{n}", [P, 2, KVG, 4, R * GD], F16) for n in range(2)]
        wk_r = [sb(f"wk_r{n}", [P, 2, KC, KVG, 4 * R, GD], F16) for n in range(2)]
        wv_g = [sb(f"wv_g{n}", [P, 2, KC, KVG * GD], F16) for n in range(2)]
        wo_g = [sb(f"wo_g{n}", [P, 2, D], F16) for n in range(2)]
        m_w = [sb(f"m_w{n}", [P, 2, H, KC, D], F16) for n in range(2)]
        wv_m = [sb(f"wv_m{n}", [P, 2, KC, INNER], F16) for n in range(2)]
        wo_m = [sb(f"wo_m{n}", [P, 2, NOC, D], F16) for n in range(2)]
        norm_w = sb("norm_w", [P, 2], F32)
        bo = sb("bo", [P, 2], F32)
        st_wq = [sb(f"st_wq{n}", [P, INNER], F32) for n in range(2)]
        st_wk = [sb(f"st_wk{n}", [P, KC, INNER], F32) for n in range(2)]
        st_wv = sb("st_wv", [P, KC, INNER], F32)
        st_wo = sb("st_wo", [P, NOC, D], F32)
        st_gq = sb("st_gq", [P, 2, D], F32)
        st_gk = sb("st_gk", [P, 2, KC, KVG * GD], F32)
        st_gv = sb("st_gv", [P, 2, KC, KVG * GD], F32)
        st_go = sb("st_go", [P, 2, D], F32)
        wq_t = sb("wq_t", [P, NOC, D], F32)
        wk_t = sb("wk_t", [P, NOC, C], F32)
        ident = sb("ident", [P, P], F32)
        ones = sb("ones", [P, 1], F32)
        minus_half = sb("minus_half", [P, 1], F32)
        part_i = sb("part_i", [P, 1], I32)
        part_f = sb("part_f", [P, 2], F32)
        head_i = sb("head_i", [P, 1], I32)
        head_mask = sb("head_mask", [P, R], F32)
        key_i = sb("key_i", [P, S], I32)
        key_f = sb("key_f", [P, S], F32)
        tok_i = sb("tok_i", [6, 4, 2], I32)
        tok_f = sb("tok_f", [6, 4, 2], F32)
        tok_w = sb("tok_w", [6, 4, 2], F32)
        hit = sb("hit", [6, 4, 2, S], F32)
        hit_any = sb("hit_any", [6, 4, S], F32)
        row_sel = sb("row_sel", [6, 8], F32)
        mask_r = sb("mask_r", [6, 8, P], F32)
        mask_p = sb("mask_p", [6, 3, P], BF16)
        bias_l = sb("bias_l", [P, P], BF16)
        bias_r = [sb(f"bias_r{n}", [P, H, S], BF16) for n in range(2)]
        x_nat = [sb(f"x_nat{n}", [P, D], F32) for n in range(STREAMS)]
        ctx_nat = [sb(f"ctx_nat{n}", [S, C], F32) for n in range(STREAMS)]
        ctx_t = [sb(f"ctx_t{n}", [P, 2, KC, S], F16) for n in range(STREAMS)]
        x_f = [sb(f"x_f{n}", [P, T], F32) for n in range(STREAMS)]
        x_b = [sb(f"x_b{n}", [P, T], F32) for n in range(STREAMS)]
        x_s = [sb(f"x_s{n}", [P, 2, T], F16) for n in range(STREAMS)]
        x_sq = [sb(f"x_sq{n}", [P, T], F32) for n in range(STREAMS)]
        y_out = [sb(f"y_out{n}", [P, D], F32) for n in range(STREAMS)]
        g_s = [sb(f"g_s{n}", [P, 2, HS], F16) for n in range(STREAMS)]
        k_bd = [sb(f"k_bd{n}", [P, KVG, R, S], F16) for n in range(STREAMS)]
        v_gqa = [sb(f"v_gqa{n}", [P, 2, KVG, GD + 1], F16) for n in range(STREAMS)]
        v_mha = [sb(f"v_mha{n}", [P, 2, H, MD + 1], F16) for n in range(STREAMS)]
        probs = [sb(f"probs{n}", [P, HS_PAD], F32) for n in range(STREAMS)]
        k_rep = sb("k_rep", [P, KVG, S], F16)
        q_rep = sb("q_rep", [P, KVG, T], F16)
        row_max = sb("row_max", [P, H], F32)
        ms = sb("ms", [P, STREAMS], F32)
        rstd = sb("rstd", [P, STREAMS], F32)
        shifted = sb("shifted", [P, H, S], F32)
        p_t = sb("p_t", [P, 2, H, T], F16)
        den_r = sb("den_r", [P, 3 * HEADS_O], F32)
        o_n = sb("o_n", [P, NOC, P], F32)
        o_t = sb("o_t", [P, 2, NOC, T], F16)
        x_res = sb("x_res", [P, D], F32)

        so = ps("so", [P, 3, BANK])
        ring_c = ps("ring_c", [P, 2, BANK])
        ring_t = ps("ring_t", [P, 2, BANK])
        misc = ps("misc", [P, BANK])
        so_flat = so[:, :, :].rearrange("p b n -> p (b n)")
        s_view = so_flat[:, 0:HS].rearrange("p (h s) -> p h s", s=S)
        SS_COL = HS + 64

        sems = {name: sem(name) for name in PER_ITEM}
        load_x = [sem(f"load_x{n}") for n in range(STREAMS)]
        load_c = [sem(f"load_c{n}") for n in range(STREAMS)]
        stored = [sem(f"stored{n}") for n in range(STREAMS)]
        load_small = sem("load_small")
        load_qk = [sem(f"load_qk{n}") for n in range(2)]
        load_vo = [sem(f"load_vo{n}") for n in range(2)]
        vo_free = sem("vo_free")
        consts_pool = sem("consts_pool")
        pool_step = sem("pool_step")
        dve_step = sem("dve_step")
        act_split = sem("act_split")
        dve_ready = sem("dve_ready")
        prep_raw = sem("prep_raw")
        prep_hi = sem("prep_hi")
        prep_free = sem("prep_free")

        NTQ = NOC // 4
        NTK = NOC * KC // 4
        NMM = H * KC // 4
        PREP = NTQ + NTK + NMM

        block = ctx.enter_context(nc.Block())

        @block.sync
        def _(sp):
            n_small = 0
            for row, d in ((0, mask_a_d), (3, mask_b_d)):
                sp.dma_start(mask_r[row:row + 3, 0, :],
                             d.rearrange("(a t) -> a t", a=1).to_broadcast([3, T])).then_inc(load_small, 16)
                n_small += 1
            for n in range(2):
                for row, d in ((0, mha_w[n]["tok_a"]), (3, mha_w[n]["tok_b"])):
                    sp.dma_start(tok_i[row:row + 3, 2 * n, :],
                                 d.rearrange("(a t) -> a t", a=1).to_broadcast([3, 2])).then_inc(load_small, 16)
                sp.dma_start(tok_i[0:6, 2 * n + 1, :],
                             mha_w[n]["tok_b"].rearrange("(a t) -> a t", a=1).to_broadcast([6, 2])).then_inc(load_small, 16)
                sp.dma_start(norm_w[:, n:n + 1], gqa_w[n]["norm_w"].rearrange("(p a) -> p a", a=1)).then_inc(load_small, 16)
                sp.dma_start(bo[:, n:n + 1], mha_w[n]["bo"].rearrange("(p a) -> p a", a=1)).then_inc(load_small, 16)
                sp.dma_start(st_gq[:, n, :], gqa_w[n]["wq"]).then_inc(load_small, 16)
                sp.dma_start(st_gk[:, n, :, :], gqa_w[n]["wk"].rearrange("(k p) n -> p k n", p=P)).then_inc(load_small, 16)
                sp.dma_start(st_gv[:, n, :, :], gqa_w[n]["wv"].rearrange("(k p) n -> p k n", p=P)).then_inc(load_small, 16)
                sp.dma_start(st_go[:, n, :], gqa_w[n]["wo"]).then_inc(load_small, 16)
                n_small += 9
            assert n_small == SMALL_LOADS
            for n in range(2):
                sp.dma_start(st_wq[n][:, :], mha_w[n]["Wq"]).then_inc(load_qk[n], 16)
                sp.dma_start(st_wk[n][:, :, :], mha_w[n]["Wk"].rearrange("(k p) n -> p k n", p=P)).then_inc(load_qk[n], 16)
            for st in range(STREAMS):
                sp.dma_start(x_nat[st][:, :], x_d[st, :, :]).then_inc(load_x[st], 16)
                sp.dma_start(ctx_nat[st][:, :], ctx_d[st, :, :]).then_inc(load_c[st], 16)
            for n in range(2):
                if n:
                    sp.wait_ge(vo_free, 2)
                sp.dma_start(st_wv[:, :, :], mha_w[n]["Wv"].rearrange("(k p) n -> p k n", p=P)).then_inc(load_vo[n], 16)
                sp.dma_start(st_wo[:, :, :], mha_w[n]["Wo"].rearrange("(k p) n -> p k n", p=P)).then_inc(load_vo[n], 16)

            def iteration(it, last):
                if not last:
                    for st in range(STREAMS):
                        sp.wait_ge(sems["x_in"], at("x_in", it, st, 1))
                        sp.dma_start(x_nat[st][:, :], x_d[it * STREAMS + STREAMS + st, :, :]).then_inc(load_x[st], 16)
                        sp.wait_ge(sems["ct_raw"], at("ct_raw", it, st, 1))
                        sp.dma_start(ctx_nat[st][:, :], ctx_d[it * STREAMS + STREAMS + st, :, :]).then_inc(load_c[st], 16)
                for st in range(STREAMS):
                    sp.wait_ge(sems["out"], at("out", it, SLOTS - STREAMS + st, 1))
                    sp.dma_start(out_d[it * STREAMS + st, :, :], y_out[st][:, :]).then_inc(stored[st], 16)

            with sp.Fori(0, NIT - 1) as it:
                iteration(it, False)
            iteration(NIT - 1, True)
            for st in range(STREAMS):
                sp.wait_ge(stored[st], 16 * NIT)

        @block.gpsimd
        def _(pool):
            pool.memset(ident[:, :], 0.0).then_inc(pool_step, 1)
            pool.memset(ones[:, :], 1.0).then_inc(consts_pool, 1)
            pool.memset(minus_half[:, :], -0.5).then_inc(consts_pool, 1)
            pool.iota(part_i[:, :], pattern=[[0, 1]], base=0, channel_multiplier=1).then_inc(consts_pool, 1)
            pool.iota(key_i[:, :], pattern=[[1, S]], base=0, channel_multiplier=0).then_inc(consts_pool, 1)
            pool.memset(bias_l[:, :], 0.0).then_inc(consts_pool, 1)
            for n in range(2):
                pool.memset(bias_r[n][:, :, :], 0.0).then_inc(consts_pool, 1)
                pool.memset(v_gqa[n][:, :, :, :], 0.0).then_inc(pool_step, 1)
                pool.memset(v_mha[n][:, :, :, :], 0.0).then_inc(pool_step, 1)
                pool.memset(probs[n][:, HS:HS_PAD], 0.0).then_inc(consts_pool, 1)
            pool.wait_ge(pool_step, 5)
            pool.affine_select(out=ident[:, :], in_=ident[:, :], compare_op=ALU.not_equal, fill=1.0, base=0,
                               pattern=[[-1, P]], channel_multiplier=1).then_inc(consts_pool, 1)
            for n in range(2):
                pool.memset(v_gqa[n][0:S, HI, :, GD:GD + 1], 1.0).then_inc(consts_pool, 1)
                pool.memset(v_mha[n][0:S, HI, :, MD:MD + 1], 1.0).then_inc(consts_pool, 1)
            pool.wait_ge(load_small, 16 * SMALL_LOADS)

            def x_parts(it, j):
                st = j % STREAMS
                pool.wait_ge(sems["x_f32"], at("x_f32", it, j, 1))
                if is_gqa(j):
                    pool.tensor_tensor(x_sq[st][:, :], x_f[st][:, :], x_f[st][:, :], ALU.mult).then_inc(sems["sq"], 1)
                pool.wait_ge(sems["x_hi"], at("x_hi", it, j, 1))
                pool.tensor_tensor(x_s[st][:, LO, :], x_f[st][:, :], x_s[st][:, HI, :], ALU.subtract).then_inc(sems["x_lo"], 1)
                if not is_gqa(j):
                    n = layer(j) // 2
                    pool.tensor_scalar(x_b[st][:, :], x_f[st][:, :], bo[:, n:n + 1], 0.0, ALU.add, ALU.add).then_inc(sems["xb"], 1)

            def slot(it, j, last=False):
                st = j % STREAMS
                if is_gqa(j):
                    pool.wait_ge(sems["ms"], at("ms", it, j, 1))
                    pool.tensor_tensor(rstd[:, st:st + 1], ms[:, st:st + 1], minus_half[:, :], ALU.pow).then_inc(sems["rstd"], 1)
                if exists(it, j + 1) and not (last and j == SLOTS - 1):
                    x_parts(it, j + 1)

            x_parts(0, 0)
            with pool.Fori(0, NIT - 1) as it:
                for j in range(SLOTS):
                    slot(it, j)
            for j in range(SLOTS):
                slot(NIT - 1, j, last=True)

        @block.scalar
        def _(act):
            def high(out, in_, scale):
                return act.activation(out, in_, ACT.Copy, scale=scale)

            act.wait_ge(load_small, 16 * SMALL_LOADS)
            act.wait_ge(dve_ready, 1)
            for n in range(2):
                high(wq_r[n][:, HI], st_gq[:, n, :].rearrange("p (g a e) -> p g a e", g=KVG, a=1).to_broadcast([P, KVG, 4, R * GD]), W_GQA).then_inc(act_split, 1)
                for kc in range(KC):
                    high(wk_r[n][:, HI, kc], st_gk[:, n, kc, :].rearrange("p (g a e) -> p g a e", g=KVG, a=1).to_broadcast([P, KVG, 4 * R, GD]), W_GQA).then_inc(act_split, 1)
                high(wv_g[n][:, HI], st_gv[:, n, :, :], W_V).then_inc(act_split, 1)
                high(wo_g[n][:, HI], st_go[:, n, :], W_V).then_inc(act_split, 1)
            for n in range(2):
                for c in range(NMM):
                    k = n * PREP + NTQ + NTK + c
                    act.wait_ge(prep_raw, k + 1)
                    high(m_w[n][:, HI].rearrange("p h k c -> p (h k c)")[:, c * BANK:(c + 1) * BANK], ring_t[:, k % 2, :], W_M).then_inc(prep_hi, 1)
                act.wait_ge(load_vo[n], 32)
                high(wv_m[n][:, HI], st_wv[:, :, :], W_V).then_inc(act_split, 1)
                high(wo_m[n][:, HI], st_wo[:, :, :], W_V).then_inc(act_split, 1)

            def turn_context(it, j):
                act.wait_ge(sems["ct_raw"], at("ct_raw", it, j, 1))
                high(ctx_t[j % STREAMS][:, HI], misc[:, 0:KC * S].rearrange("p (k s) -> p k s", s=S), 1.0).then_inc(sems["ct_hi"], 1)

            def context_chunk(it, j, k):
                st = j % STREAMS
                b = buffer_of("ctx_raw", j, k)
                act.wait_ge(sems["ctx_raw"], at("ctx_raw", it, j, k + 1))
                if is_gqa(j) and k == 0:
                    if exists(it, j - STREAMS):
                        prev = j - 1 if is_gqa(j - 1) else j - 1 - STREAMS
                        if exists(it, prev):
                            act.wait_ge(sems["kb"], at("kb", it, prev, 1))
                    elif j % STREAMS == 1:
                        act.wait_ge(sems["kb"], at("kb", it, j - 1, 1))
                    ins = high(k_rep[:, :, :], ring_c[:, b, 0:KVG * S].rearrange("p (g s) -> p g s", s=S), 1.0)
                elif is_gqa(j):
                    ins = high(v_gqa[st][0:S, HI, :, 0:GD], ring_c[0:S, b, 0:KVG * GD].rearrange("p (g d) -> p g d", d=GD), 1.0)
                elif k < len(G_CHUNKS):
                    h0, h1 = G_CHUNKS[k]
                    ins = high(g_s[st][:, HI, h0 * S:h1 * S], ring_c[:, b, 0:(h1 - h0) * S], 1.0)
                else:
                    n0, n1 = V_CHUNKS[k - len(G_CHUNKS)]
                    ins = high(v_mha[st][0:S, HI, n0 // MD:n1 // MD, 0:MD], ring_c[0:S, b, :].rearrange("p (h d) -> p h d", d=MD), 1.0)
                ins.then_inc(sems["ctx_hi"], 1)

            def turned(it, j, k):
                b = buffer_of("flip_raw", j, k)
                act.wait_ge(sems["flip_raw"], at("flip_raw", it, j, k + 1))
                if k < NTURN:
                    ins = high(p_t[:, HI, k * TURN:(k + 1) * TURN, :], ring_t[:, b, :].rearrange("p (h t) -> p h t", t=T), W_P)
                elif is_gqa(j):
                    ins = high(o_t[:, HI, 0, :], ring_t[:, b, 0:T], 1.0)
                else:
                    c = (k - NTURN) * TURN
                    ins = high(o_t[:, HI, c:c + TURN, :], ring_t[:, b, :].rearrange("p (h t) -> p h t", t=T), 1.0)
                ins.then_inc(sems["flip_hi"], 1)

            def x_high(it, j):
                st = j % STREAMS
                act.wait_ge(sems["x_f32"], at("x_f32", it, j, 1))
                high(x_s[st][:, HI, :], x_f[st][:, :], 1.0).then_inc(sems["x_hi"], 1)

            def slot(it, j, last=False):
                st = j % STREAMS
                p, c = j - 1, j + 1
                post, more = exists(it, p), not (last and j == SLOTS - 1)
                chunks = list(range(PER_ITEM["ctx_raw"][layer(c)])) if more else []
                if is_gqa(j):
                    act.wait_ge(sems["q_raw"], at("q_raw", it, j, 1))
                    high(q_rep[:, :, :], misc[:, :].rearrange("p (g t) -> p g t", t=T), 1.0).then_inc(sems["q_hi"], 1)
                if post:
                    turned(it, p, 0)
                    turned(it, p, 1)
                if chunks:
                    context_chunk(it, c, chunks.pop(0))
                act.wait_ge(sems["s_sub"], at("s_sub", it, j, 1))
                if is_gqa(j):
                    act.wait_ge(sems["rstd"], at("rstd", it, j, 1))
                    act.activation(probs[st][:, 0:HS], shifted[:, :, :].rearrange("p h s -> p (h s)"), ACT.Exp,
                                   scale=rstd[:, st:st + 1]).then_inc(sems["p_exp"], 1)
                else:
                    act.activation(probs[st][:, 0:HS], shifted[:, :, :].rearrange("p h s -> p (h s)"), ACT.Exp,
                                   scale=MHA_SCALE).then_inc(sems["p_exp"], 1)
                if chunks:
                    context_chunk(it, c, chunks.pop(0))
                if post and layer(p) == LAYERS - 1:
                    act.wait_ge(sems["xr_raw"], at("xr_raw", it, p, 1))
                    high(x_res[:, :], misc[:, 0:D], 1.0).then_inc(sems["xr"], 1)
                if post:
                    turned(it, p, 2)
                if more and layer(c) == 0:
                    x_high(it, c)
                if post:
                    turned(it, p, 3)
                if chunks:
                    context_chunk(it, c, chunks.pop(0))
                if layer(j + 2) == 0 and (not last or j + 2 < SLOTS):
                    turn_context(it, j + 2)
                if chunks:
                    context_chunk(it, c, chunks.pop(0))
                if post:
                    for k in range(NTURN, PER_ITEM["flip_raw"][layer(p)]):
                        turned(it, p, k)
                if chunks:
                    context_chunk(it, c, chunks.pop(0))
                if more and layer(c) > 0:
                    x_high(it, c)

            turn_context(0, 0)
            for k in range(PER_ITEM["ctx_raw"][0]):
                context_chunk(0, 0, k)
            turn_context(0, 1)
            x_high(0, 0)
            for j in range(SLOTS):
                slot(0, j)
            with act.Fori(1, NIT - 1) as it:
                for j in range(SLOTS):
                    slot(it, j)
            for j in range(SLOTS):
                slot(NIT - 1, j, last=True)
            j = SLOTS - 1
            act.wait_ge(sems["xr_raw"], at("xr_raw", NIT - 1, j, 1))
            high(x_res[:, :], misc[:, 0:D], 1.0).then_inc(sems["xr"], 1)
            for k in range(PER_ITEM["flip_raw"][layer(j)]):
                turned(NIT - 1, j, k)

        @block.vector
        def _(dve):
            def low(out, in_, scale, hi):
                return dve.scalar_tensor_tensor(out=out, in0=in_, scalar=scale, in1=hi, op0=ALU.mult, op1=ALU.subtract)

            steps = [0]

            def step(ins):
                steps[0] += 1
                ins.then_inc(dve_step, 1)
                dve.wait_ge(dve_step, steps[0])

            N_CONST = 14
            dve.wait_ge(consts_pool, N_CONST)
            dve.wait_ge(load_small, 16 * SMALL_LOADS)
            for n in range(2):
                step(dve.tensor_scalar(st_gq[:, n, :], st_gq[:, n, :], norm_w[:, n:n + 1], None, ALU.mult))
            step(dve.tensor_copy(part_f[:, 0:1], part_i[:, :]))
            dve.tensor_copy(key_f[:, :], key_i[:, :]).then_inc(dve_ready, 1)
            step(dve.tensor_scalar(head_i[:, :], part_i[:, :], int(np.log2(GD)), R - 1, ALU.logical_shift_right, ALU.bitwise_and))
            step(dve.tensor_copy(part_f[:, 1:2], head_i[:, :]))
            for r in range(R):
                step(dve.tensor_scalar(head_mask[:, r:r + 1], part_f[:, 1:2], float(r), None, ALU.is_equal))
            for k in range(3):
                step(dve.tensor_scalar(row_sel[:, k:k + 1], part_f[0:6, 0:1], float(k), None, ALU.is_equal))
                step(dve.tensor_scalar(row_sel[:, 4:5], part_f[0:6, 0:1], float(k + 3), None, ALU.is_equal))
                step(dve.tensor_tensor(row_sel[:, k:k + 1], row_sel[:, k:k + 1], row_sel[:, 4:5], ALU.add))
            step(dve.tensor_scalar(row_sel[:, 3:4], part_f[0:6, 0:1], 3.0, None, ALU.is_lt))
            tok_flat = tok_f[:, :, :].rearrange("p a b -> p (a b)")
            wrap_flat = tok_w[:, :, :].rearrange("p a b -> p (a b)")
            step(dve.tensor_copy(tok_flat, tok_i[:, :, :].rearrange("p a b -> p (a b)")))
            step(dve.tensor_scalar(wrap_flat, tok_flat, 0.0, float(S), ALU.is_lt, ALU.mult))
            step(dve.tensor_tensor(tok_flat, tok_flat, wrap_flat, ALU.add))
            for a in range(4):
                for b in range(2):
                    step(dve.tensor_scalar(hit[:, a, b, :], key_f[0:6, :], tok_f[:, a, b:b + 1], None, ALU.is_equal))
                step(dve.tensor_tensor(hit_any[:, a, :], hit[:, a, 0, :], hit[:, a, 1, :], ALU.max))
            for n in range(2):
                own, over = hit_any[:, 2 * n, :], hit_any[:, 2 * n + 1, :]
                step(dve.tensor_scalar(over, over, row_sel[:, 3:4], -1.0, ALU.mult, ALU.mult))
                step(dve.tensor_scalar(over, over, 1.0, None, ALU.add))
                step(dve.tensor_tensor(own, own, over, ALU.mult))
                step(dve.tensor_copy(bias_r[n][0:6, :, :], own.unsqueeze(1).to_broadcast([6, H, S])))
            m = [mask_r[:, k, :] for k in range(8)]
            step(dve.tensor_scalar(m[1], m[0], -1.0, 1.0, ALU.mult, ALU.add))
            step(dve.tensor_scalar(m[2], m[1], -SUPPRESS, 1.0 / MHA_SCALE, ALU.mult, ALU.mult))
            step(dve.tensor_copy(mask_p[:, 0, :], m[2]))
            step(dve.tensor_tensor(m[3], m[2], mask_p[:, 0, :], ALU.subtract))
            step(dve.tensor_copy(mask_p[:, 1, :], m[3]))
            step(dve.tensor_tensor(m[4], m[3], mask_p[:, 1, :], ALU.subtract))
            step(dve.tensor_copy(mask_p[:, 2, :], m[4]))
            step(dve.tensor_scalar(m[5], mask_p[:, 0, :], row_sel[:, 0:1], None, ALU.mult))
            step(dve.scalar_tensor_tensor(out=m[6], in0=mask_p[:, 1, :], scalar=row_sel[:, 1:2], in1=m[5], op0=ALU.mult, op1=ALU.add))
            step(dve.scalar_tensor_tensor(out=bias_l[0:6, :], in0=mask_p[:, 2, :], scalar=row_sel[:, 2:3], in1=m[6], op0=ALU.mult, op1=ALU.add))

            assert steps[0] == DVE_STEPS, steps[0]

            NSPLIT = 3 + KC
            for n in range(2):
                dve.wait_ge(act_split, NSPLIT * (n + 1))
                for g in range(KVG):
                    low(wq_r[n][:, LO, g], st_gq[:, n, g * R * GD:(g + 1) * R * GD].unsqueeze(1).to_broadcast([P, 4, R * GD]), W_GQA, wq_r[n][:, HI, g]).then_inc(dve_ready, 1)
                for kc in range(KC):
                    for g in range(KVG):
                        low(wk_r[n][:, LO, kc, g], st_gk[:, n, kc, g * GD:(g + 1) * GD].unsqueeze(1).to_broadcast([P, 4 * R, GD]), W_GQA, wk_r[n][:, HI, kc, g]).then_inc(dve_ready, 1)
                low(wv_g[n][:, LO], st_gv[:, n, :, :], W_V, wv_g[n][:, HI]).then_inc(dve_ready, 1)
                low(wo_g[n][:, LO], st_go[:, n, :], W_V, wo_g[n][:, HI]).then_inc(dve_ready, 1)
            for n in range(2):
                for c in range(NTQ + NTK):
                    k = n * PREP + c
                    dve.wait_ge(prep_raw, k + 1)
                    dst = (wq_t[:, :, :] if c < NTQ else wk_t[:, :, :]).rearrange("p a b -> p (a b)")
                    o = (c if c < NTQ else c - NTQ) * BANK
                    dve.tensor_copy(dst[:, o:o + BANK], ring_t[:, k % 2, :]).then_inc(prep_free, 1)
                for c in range(NMM):
                    k = n * PREP + NTQ + NTK + c
                    dve.wait_ge(prep_hi, n * NMM + c + 1)
                    part = slice(c * BANK, (c + 1) * BANK)
                    low(m_w[n][:, LO].rearrange("p h k c -> p (h k c)")[:, part], ring_t[:, k % 2, :], W_M,
                        m_w[n][:, HI].rearrange("p h k c -> p (h k c)")[:, part]).then_inc(prep_free, 1)
                dve.wait_ge(act_split, 2 * NSPLIT + 2 * (n + 1))
                low(wv_m[n][:, LO], st_wv[:, :, :], W_V, wv_m[n][:, HI]).then_inc(vo_free, 1)
                low(wo_m[n][:, LO], st_wo[:, :, :], W_V, wo_m[n][:, HI]).then_inc(vo_free, 1)

            def turn_context(it, j):
                st = j % STREAMS
                dve.wait_ge(sems["ct_hi"], at("ct_hi", it, j, 1))
                low(ctx_t[st][:, LO], misc[:, 0:KC * S].rearrange("p (k s) -> p k s", s=S), 1.0, ctx_t[st][:, HI]).then_inc(sems["ct_lo"], 1)

            def context_chunk(it, j, k):
                st = j % STREAMS
                b = buffer_of("ctx_raw", j, k)
                dve.wait_ge(sems["ctx_hi"], at("ctx_hi", it, j, k + 1))
                if is_gqa(j) and k == 0:
                    raw = ring_c[:, b, 0:KVG * S].rearrange("p (g s) -> p g s", s=S)
                    low(k_rep[32:64], raw[32:64], 1.0, k_rep[32:64])
                    low(k_rep[96:128], raw[96:128], 1.0, k_rep[96:128]).then_inc(sems["ctx_lo"], 1)
                    dve.wait_ge(sems["ctx_lo"], at("ctx_lo", it, j, 1))
                    for r in range(R):
                        ins = dve.tensor_scalar(k_bd[st][:, :, r, :], k_rep[:, :, :], head_mask[:, r:r + 1], None, ALU.mult)
                    ins.then_inc(sems["kb"], 1)
                    return
                if is_gqa(j):
                    v = v_gqa[st]
                    ins = low(v[0:S, LO, :, 0:GD], ring_c[0:S, b, 0:KVG * GD].rearrange("p (g d) -> p g d", d=GD), 1.0, v[0:S, HI, :, 0:GD])
                elif k < len(G_CHUNKS):
                    h0, h1 = G_CHUNKS[k]
                    ins = low(g_s[st][:, LO, h0 * S:h1 * S], ring_c[:, b, 0:(h1 - h0) * S], 1.0, g_s[st][:, HI, h0 * S:h1 * S])
                else:
                    n0, n1 = V_CHUNKS[k - len(G_CHUNKS)]
                    v, hs = v_mha[st], slice(n0 // MD, n1 // MD)
                    ins = low(v[0:S, LO, hs, 0:MD], ring_c[0:S, b, :].rearrange("p (h d) -> p h d", d=MD), 1.0, v[0:S, HI, hs, 0:MD])
                ins.then_inc(sems["ctx_lo"], 1)

            def turned(it, j, k):
                b = buffer_of("flip_raw", j, k)
                dve.wait_ge(sems["flip_hi"], at("flip_hi", it, j, k + 1))
                if k < NTURN:
                    hs = slice(k * TURN, (k + 1) * TURN)
                    ins = low(p_t[:, LO, hs, :], ring_t[:, b, :].rearrange("p (h t) -> p h t", t=T), W_P, p_t[:, HI, hs, :])
                elif is_gqa(j):
                    ins = low(o_t[:, LO, 0, :], ring_t[:, b, 0:T], 1.0, o_t[:, HI, 0, :])
                else:
                    cs = slice((k - NTURN) * TURN, (k - NTURN + 1) * TURN)
                    ins = low(o_t[:, LO, cs, :], ring_t[:, b, :].rearrange("p (h t) -> p h t", t=T), 1.0, o_t[:, HI, cs, :])
                ins.then_inc(sems["flip_lo"], 1)

            def normalise(it, j, k):
                dve.wait_ge(sems["o_raw"], at("o_raw", it, j, k + 1))
                if is_gqa(j):
                    o = so_flat[:, 0:H * (GD + 1)].rearrange("p (h d) -> p h d", d=GD + 1)
                    r = den_r[:, 0:H].unsqueeze(2)
                    dst, width = o_n[:, 0, :].rearrange("p (h d) -> p h d", d=GD), [P, H, GD]
                    num, den = o[:, :, 0:GD], o[:, :, GD:GD + 1]
                else:
                    b0, nb, nh = ((0, 2, HEADS_O), (2, 1, H - 2 * HEADS_O))[k]
                    o = so[:, b0:b0 + nb, 0:nh * (MD + 1)].rearrange("p b (h d) -> p b h d", d=MD + 1)
                    h0 = b0 * HEADS_O
                    r = den_r[:, h0:h0 + nb * nh].rearrange("p (b h a) -> p b h a", h=nh, a=1)
                    dst = o_n[:, :, :].rearrange("p c (a d) -> p (c a d)", d=MD)[:, h0 * MD:(h0 + nb * nh) * MD].rearrange("p (b h d) -> p b h d", h=nh, d=MD)
                    num, den, width = o[:, :, :, 0:MD], o[:, :, :, MD:MD + 1], [P, nb, nh, MD]
                dve.reciprocal(r, den).then_inc(sems["o_rcp"], 1)
                dve.wait_ge(sems["o_rcp"], at("o_rcp", it, j, k + 1))
                dve.tensor_tensor(dst, num, r.to_broadcast(width), ALU.mult).then_inc(sems["o_norm"], 1)

            def first_x(it, j):
                dve.wait_ge(sems["x_in"], at("x_in", it, j, 1))
                dve.tensor_copy(x_f[j % STREAMS][:, :], misc[:, 0:T]).then_inc(sems["x_f32"], 1)

            def finish(it, p):
                st = p % STREAMS
                dve.wait_ge(sems["y_raw"], at("y_raw", it, p, 1))
                if layer(p) == LAYERS - 1:
                    dve.wait_ge(sems["xr"], at("xr", it, p, 1))
                    if exists(it, p - SLOTS):
                        dve.wait_ge(stored[st], 16 * (it + p // SLOTS))
                    dve.scalar_tensor_tensor(out=y_out[st][:, :], in0=misc[:, 0:D], scalar=Y_SCALE, in1=x_res[:, :],
                                             op0=ALU.mult, op1=ALU.add).then_inc(sems["out"], 1)
                    return
                base = x_f[st]
                if not is_gqa(p):
                    dve.wait_ge(sems["xb"], at("xb", it, p, 1))
                    base = x_b[st]
                dve.scalar_tensor_tensor(out=x_f[st][:, :], in0=misc[:, 0:T], scalar=Y_SCALE, in1=base[:, :],
                                         op0=ALU.mult, op1=ALU.add).then_inc(sems["x_f32"], 1)

            def slot(it, j, last=False):
                st = j % STREAMS
                p, c = j - 1, j + 1
                post, more = exists(it, p), not (last and j == SLOTS - 1)
                chunks = list(range(PER_ITEM["ctx_raw"][layer(c)])) if more else []
                if is_gqa(j):
                    dve.wait_ge(sems["q_hi"], at("q_hi", it, j, 1))
                    low(q_rep[64:128], misc[64:128, :].rearrange("p (g t) -> p g t", t=T), 1.0, q_rep[64:128]).then_inc(sems["q_lo"], 1)
                if post:
                    turned(it, p, 0)
                    turned(it, p, 1)
                dve.wait_ge(sems["s_raw"], at("s_raw", it, j, 1))
                if is_gqa(j):
                    dve.tensor_scalar(ms[:, st:st + 1], so_flat[:, SS_COL:SS_COL + 1], SS_MUL, SS_ADD, ALU.mult, ALU.add).then_inc(sems["ms"], 1)
                dve.tensor_reduce(row_max[:, :], s_view, AX_X, ALU.max).then_inc(sems["s_max"], 1)
                dve.wait_ge(sems["s_max"], at("s_max", it, j, 1))
                if exists(it, j - 1):
                    dve.wait_ge(sems["p_exp"], at("p_exp", it, j - 1, 1))
                dve.tensor_tensor(shifted[:, :, :], s_view, row_max[:, :].unsqueeze(2).to_broadcast([P, H, S]), ALU.subtract).then_inc(sems["s_sub"], 1)
                for _ in range(2):
                    if chunks:
                        context_chunk(it, c, chunks.pop(0))
                if post:
                    turned(it, p, 2)
                if more and layer(c) == 0:
                    first_x(it, c)
                if post:
                    turned(it, p, 3)
                if chunks:
                    context_chunk(it, c, chunks.pop(0))
                if layer(j + 2) == 0 and (not last or j + 2 < SLOTS):
                    turn_context(it, j + 2)
                if post:
                    for k in range(PER_ITEM["o_raw"][layer(p)]):
                        normalise(it, p, k)
                if chunks:
                    context_chunk(it, c, chunks.pop(0))
                if post:
                    for k in range(NTURN, PER_ITEM["flip_raw"][layer(p)]):
                        turned(it, p, k)
                if chunks:
                    context_chunk(it, c, chunks.pop(0))
                if post:
                    finish(it, p)

            turn_context(0, 0)
            for k in range(PER_ITEM["ctx_raw"][0]):
                context_chunk(0, 0, k)
            turn_context(0, 1)
            first_x(0, 0)
            for j in range(SLOTS):
                slot(0, j)
            with dve.Fori(1, NIT - 1) as it:
                for j in range(SLOTS):
                    slot(it, j)
            for j in range(SLOTS):
                slot(NIT - 1, j, last=True)
            j = SLOTS - 1
            for k in range(NTURN):
                turned(NIT - 1, j, k)
            for k in range(2):
                normalise(NIT - 1, j, k)
            for k in range(NTURN, NTURN + NOT):
                turned(NIT - 1, j, k)
            finish(NIT - 1, j)

        @block.tensor
        def _(pe):
            def split_product(out, terms):
                passes = [(a[x], b[y]) for a, b in terms for x, y in ((HI, HI), (HI, LO), (LO, HI))]
                for n, (a, b) in enumerate(passes):
                    ins = pe.matmul(out, a, b, start=(n == 0), stop=(n == len(passes) - 1))
                return ins

            def hl(f):
                return f(HI), f(LO)

            pe.wait_ge(consts_pool, 14)
            for n in range(2):
                pe.wait_ge(load_qk[n], 32)
                k = n * PREP
                blocks = [(st_wq[n][:, c * P:(c + 1) * P]) for c in range(NOC)]
                blocks += [(st_wk[n][:, kc, c * P:(c + 1) * P]) for c in range(NOC) for kc in range(KC)]
                for q in range(0, len(blocks), 4):
                    if k >= 2:
                        pe.wait_ge(prep_free, k - 1)
                    for m in range(4):
                        ins = pe.transpose(ring_t[:, k % 2, m * P:(m + 1) * P], blocks[q + m], ident[:, :])
                    ins.then_inc(prep_raw, 1)
                    k += 1
                pe.wait_ge(prep_free, n * PREP + NTQ + NTK)
                for q in range(0, H * KC, 4):
                    pe.wait_ge(prep_free, k - 1)
                    for m in range(4):
                        place, kc = divmod(q + m, KC)
                        r, pair = place // NOC * MD, place % NOC
                        ins = pe.matmul(ring_t[:, k % 2, m * P:(m + 1) * P], wk_t[r:r + MD, pair, kc * P:(kc + 1) * P],
                                        wq_t[r:r + MD, pair, :], start=True, stop=True)
                    ins.then_inc(prep_raw, 1)
                    k += 1
            pe.wait_ge(prep_free, 2 * PREP)
            pe.wait_ge(vo_free, 4)
            pe.wait_ge(dve_ready, 1 + 2 * (KVG + KC * KVG + 2))
            pe.wait_ge(dve_step, DVE_STEPS)

            def turn_context(it, j):
                st = j % STREAMS
                pe.wait_ge(load_c[st], 16 * (it + j // SLOTS + 1))
                for kc in range(KC):
                    ins = pe.transpose(misc[:, kc * S:(kc + 1) * S], ctx_nat[st][:, kc * P:(kc + 1) * P], ident[0:S, 0:S])
                ins.then_inc(sems["ct_raw"], 1)

            def turn_x(it, j):
                st = j % STREAMS
                pe.wait_ge(load_x[st], 16 * (it + j // SLOTS + 1))
                pe.transpose(misc[:, 0:T], x_nat[st][:, :], ident[:, :]).then_inc(sems["x_in"], 1)

            def context_chunk(it, j, k):
                st, n = j % STREAMS, layer(j) // 2
                b = buffer_of("ctx_raw", j, k)
                if k == 0:
                    pe.wait_ge(sems["ct_lo"], at("ct_lo", it, j if layer(j) == 0 else st + SLOTS * (j // SLOTS), 1))
                if not (isinstance(it, int) and at("ctx_raw", it, j, k) < 2):
                    pe.wait_ge(sems["ctx_lo"], at("ctx_lo", it, j, k) - 1)
                ct = ctx_t[st]
                if is_gqa(j) and k == 0:
                    for g in range(KVG):
                        ins = split_product(ring_c[:, b, g * S:(g + 1) * S],
                                            [(hl(lambda i: wk_r[n][:, i, kc, g].rearrange("p a d -> p (a d)")), hl(lambda i: ct[:, i, kc, :]))
                                             for kc in range(KC)])
                elif is_gqa(j):
                    ins = split_product(ring_c[0:S, b, 0:KVG * GD],
                                        [(hl(lambda i: ct[:, i, kc, :]), hl(lambda i: wv_g[n][:, i, kc, :])) for kc in range(KC)])
                elif k < len(G_CHUNKS):
                    h0, h1 = G_CHUNKS[k]
                    for h in range(h0, h1):
                        ins = split_product(ring_c[:, b, (h - h0) * S:(h - h0 + 1) * S],
                                            [(hl(lambda i: m_w[n][:, i, m_place(h), kc, :]), hl(lambda i: ct[:, i, kc, :])) for kc in range(KC)])
                else:
                    n0, n1 = V_CHUNKS[k - len(G_CHUNKS)]
                    ins = split_product(ring_c[0:S, b, :],
                                        [(hl(lambda i: ct[:, i, kc, :]), hl(lambda i: wv_m[n][:, i, kc, n0:n1])) for kc in range(KC)])
                ins.then_inc(sems["ctx_raw"], 1)

            def ring_t_free(it, j, k):
                if not (isinstance(it, int) and at("flip_raw", it, j, k) < 2):
                    pe.wait_ge(sems["flip_lo"], at("flip_lo", it, j, k) - 1)

            def turn_probs(it, j, k):
                if k == 0:
                    pe.wait_ge(sems["p_exp"], at("p_exp", it, j, 1))
                ring_t_free(it, j, k)
                b = buffer_of("flip_raw", j, k)
                for m in range(TURN):
                    h = k * TURN + m
                    ins = pe.transpose(ring_t[:, b, m * T:(m + 1) * T], probs[j % STREAMS][:, h * S:h * S + P], ident[:, :])
                ins.then_inc(sems["flip_raw"], 1)

            def values(it, j, k):
                st = j % STREAMS
                pe.wait_ge(sems["flip_lo"], at("flip_lo", it, j, k + 1))
                for h in range(k * TURN, (k + 1) * TURN):
                    if is_gqa(j):
                        out, v = so_flat[:, h * (GD + 1):(h + 1) * (GD + 1)], hl(lambda i: v_gqa[st][:, i, h // R, :])
                    else:
                        o = (h % HEADS_O) * (MD + 1)
                        out, v = so[:, h // HEADS_O, o:o + MD + 1], hl(lambda i: v_mha[st][:, i, h, :])
                    ins = split_product(out, [(hl(lambda i: p_t[:, i, h, :]), v)])
                if k == NTURN - 1 or (k == NTURN - 2 and not is_gqa(j)):
                    ins.then_inc(sems["o_raw"], 1)

            def turn_o(it, j, k):
                if k == 0:
                    pe.wait_ge(sems["o_norm"], at("o_norm", it, j, PER_ITEM["o_norm"][layer(j)]))
                ring_t_free(it, j, NTURN + k)
                b = buffer_of("flip_raw", j, NTURN + k)
                for m in range(1 if is_gqa(j) else TURN):
                    ins = pe.transpose(ring_t[:, b, m * T:(m + 1) * T], o_n[:, k * TURN + m, :], ident[:, :])
                ins.then_inc(sems["flip_raw"], 1)

            def output(it, j):
                n = layer(j) // 2
                pe.wait_ge(sems["flip_lo"], at("flip_lo", it, j, PER_ITEM["flip_lo"][layer(j)]))
                if is_gqa(j):
                    terms = [(hl(lambda i: wo_g[n][:, i, :]), hl(lambda i: o_t[:, i, 0, :]))]
                else:
                    terms = [(hl(lambda i: wo_m[n][:, i, c, :]), hl(lambda i: o_t[:, i, c, :])) for c in range(NOC)]
                if layer(j) == LAYERS - 1:
                    terms = [(b, a) for a, b in terms]
                split_product(misc[:, 0:P], terms).then_inc(sems["y_raw"], 1)

            def scores(it, j):
                st, n = j % STREAMS, layer(j) // 2
                if exists(it, j - 2):
                    pe.wait_ge(sems["o_norm"], at("o_norm", it, j - 2, PER_ITEM["o_norm"][layer(j - 2)]))
                if is_gqa(j):
                    pe.wait_ge(sems["sq"], at("sq", it, j, 1))
                    pe.matmul(so_flat[:, SS_COL:SS_COL + 1], x_sq[st][:, :], ones[:, :], start=True, stop=True)
                    pe.wait_ge(sems["kb"], at("kb", it, j, 1))
                    pe.wait_ge(sems["q_lo"], at("q_lo", it, j, 1))
                    kb = k_bd[st][:, :, :, :].rearrange("p g r s -> p (g r s)")
                    for g in range(KVG):
                        a = g * R * S
                        while a < (g + 1) * R * S:
                            e = min((g + 1) * R * S, (a // BANK + 1) * BANK)
                            ins = pe.matmul(so_flat[:, a:e], q_rep[:, g, :], kb[:, a:e], start=True, stop=True)
                            a = e
                else:
                    pe.wait_ge(sems["x_lo"], at("x_lo", it, j, 1))
                    pe.wait_ge(sems["ctx_lo"], at("ctx_lo", it, j, len(G_CHUNKS)))
                    ind = bias_r[n][:, :, :].rearrange("p h s -> p (h s)")
                    for a in range(0, HS, BANK):
                        e = min(HS, a + BANK)
                        pe.matmul(so_flat[:, a:e], bias_l[:, :], ind[:, a:e], start=True, stop=False)
                        for x, y in ((HI, HI), (HI, LO), (LO, HI)):
                            ins = pe.matmul(so_flat[:, a:e], x_s[st][:, x, :], g_s[st][:, y, a:e], start=False, stop=(x == LO))
                ins.then_inc(sems["s_raw"], 1)

            def queries(it, j):
                st, n = j % STREAMS, layer(j) // 2
                pe.wait_ge(sems["x_lo"], at("x_lo", it, j, 1))
                for g in range(KVG):
                    ins = split_product(misc[:, g * T:(g + 1) * T],
                                        [(hl(lambda i: wq_r[n][:, i, g].rearrange("p a d -> p (a d)")), hl(lambda i: x_s[st][:, i, :]))])
                ins.then_inc(sems["q_raw"], 1)

            def slot(it, j, last=False):
                p, c = j - 1, j + 1
                post, more = exists(it, p), not (last and j == SLOTS - 1)
                chunks = list(range(PER_ITEM["ctx_raw"][layer(c)])) if more else []
                if exists(it, j - 2):
                    if layer(j - 2) == LAYERS - 1:
                        pe.wait_ge(sems["out"], at("out", it, j - 2, 1))
                    else:
                        pe.wait_ge(sems["x_f32"], at("x_f32", it, j, 1))
                if isinstance(it, int) and it == 0 and j == 0:
                    pe.wait_ge(sems["x_f32"], at("x_f32", it, j, 1))
                if isinstance(it, int) and it == 0 and j == 1:
                    pe.wait_ge(sems["x_f32"], at("x_f32", it, j, 1))
                if is_gqa(j):
                    queries(it, j)
                if post:
                    turn_probs(it, p, 0)
                    turn_probs(it, p, 1)
                scores(it, j)
                for _ in range(2):
                    if chunks:
                        context_chunk(it, c, chunks.pop(0))
                if is_gqa(j):
                    misc_free = ("q_lo", j)
                else:
                    misc_free = None
                if post and layer(p) == LAYERS - 1:
                    if misc_free:
                        pe.wait_ge(sems[misc_free[0]], at(misc_free[0], it, misc_free[1], 1))
                    pe.wait_ge(sems["xb"], at("xb", it, p, 1))
                    pe.transpose(misc[:, 0:D], x_b[p % STREAMS][:, :], ident[:, :]).then_inc(sems["xr_raw"], 1)
                    misc_free = ("xr", p)
                pe.wait_ge(sems["s_sub"], at("s_sub", it, j, 1))
                if post:
                    values(it, p, 0)
                    turn_probs(it, p, 2)
                if more and layer(c) == 0:
                    if misc_free:
                        pe.wait_ge(sems[misc_free[0]], at(misc_free[0], it, misc_free[1], 1))
                    turn_x(it, c)
                    misc_free = ("x_f32", c)
                if post:
                    values(it, p, 1)
                    turn_probs(it, p, 3)
                if chunks:
                    context_chunk(it, c, chunks.pop(0))
                if layer(j + 2) == 0 and (not last or j + 2 < SLOTS):
                    if misc_free:
                        pe.wait_ge(sems[misc_free[0]], at(misc_free[0], it, misc_free[1], 1))
                    turn_context(it, j + 2)
                    misc_free = ("ct_lo", j + 2)
                if post:
                    values(it, p, 2)
                    values(it, p, 3)
                if chunks:
                    context_chunk(it, c, chunks.pop(0))
                if post:
                    for k in range(PER_ITEM["flip_raw"][layer(p)] - NTURN):
                        turn_o(it, p, k)
                if chunks:
                    context_chunk(it, c, chunks.pop(0))
                if post:
                    if misc_free:
                        pe.wait_ge(sems[misc_free[0]], at(misc_free[0], it, misc_free[1], 1))
                    output(it, p)

            turn_context(0, 0)
            for k in range(PER_ITEM["ctx_raw"][0]):
                context_chunk(0, 0, k)
            turn_context(0, 1)
            pe.wait_ge(sems["ct_lo"], at("ct_lo", 0, 1, 1))
            turn_x(0, 0)
            for j in range(SLOTS):
                slot(0, j)
            with pe.Fori(1, NIT - 1) as it:
                for j in range(SLOTS):
                    slot(it, j)
            for j in range(SLOTS):
                slot(NIT - 1, j, last=True)
            it, j = NIT - 1, SLOTS - 1
            pe.wait_ge(sems["out"], at("out", it, j - 1, 1))
            pe.wait_ge(sems["xb"], at("xb", it, j, 1))
            pe.transpose(misc[:, 0:D], x_b[j % STREAMS][:, :], ident[:, :]).then_inc(sems["xr_raw"], 1)
            turn_probs(it, j, 0)
            turn_probs(it, j, 1)
            values(it, j, 0)
            turn_probs(it, j, 2)
            values(it, j, 1)
            turn_probs(it, j, 3)
            values(it, j, 2)
            values(it, j, 3)
            for k in range(NOT):
                turn_o(it, j, k)
            pe.wait_ge(sems["xr"], at("xr", it, j, 1))
            output(it, j)


SMALL_LOADS = 20
DVE_STEPS = 52


_GQA = ("wq", "wk", "wv", "wo", "norm_w")
_MHA = {"Wq": "Wq", "Wk": "Wk", "Wv": "Wv", "Wo": "Wo", "bo": "bo",
        "tok_a": "token_indices_A", "tok_b": "token_indices_B"}


def kernel(**inputs):
    import numpy as _np
    import concourse.bacc as _bacc
    from concourse import mybir as _mybir
    from concourse.bass_utils import run_bass_kernel_spmd as _run

    nc = _bacc.Bacc("TRN2", target_bir_lowering=False, num_devices=1)
    arrays = {}

    def given(name):
        a = _np.ascontiguousarray(inputs[name])
        arrays[f"in_{name}_dram"] = a
        return nc.dram_tensor(f"in_{name}_dram", a.shape, _mybir.dt.from_np(a.dtype), kind="ExternalInput").ap()

    x, ctx = given("x"), given("ctx_2048")
    mask_a, mask_b = given("mask_S_fk1"), given("mask_S_fk0")
    gqa = [{k: given(f"L{n}_xattn_{k}") for k in _GQA} for n in (0, 2)]
    mha = [{k: given(f"L{n}_xattn_{v}") for k, v in _MHA.items()} for n in (1, 3)]
    out = nc.dram_tensor("out_0_dram", x.shape, _mybir.dt.float32, kind="ExternalOutput").ap()
    build(nc, x, ctx, mask_a, mask_b, gqa, mha, out)
    r = _run(nc, [arrays], core_ids=[0])
    return r.results[0]["out_0_dram"]
```

```python
from contextlib import ExitStack

import numpy as np

import concourse.bass as bass
from concourse import mybir

ALU = mybir.AluOpType
ACT = mybir.ActivationFunctionType
AX_X = mybir.AxisListType.X
F32 = mybir.dt.float32
F16 = mybir.dt.float16
BF16 = mybir.dt.bfloat16
I32 = mybir.dt.int32

P = 128
H = 16
EPS = 1e-5
SUPPRESS = 20.0
STREAMS = 4
LAYERS = 4
SLOTS = STREAMS * LAYERS
PLACES = [0, 3, 8, 11]
ITEMS = [next((st, la, int(2 * st + PLACES[la] >= SLOTS)) for st in range(STREAMS) for la in range(LAYERS)
              if (2 * st + PLACES[la]) % SLOTS == j) for j in range(SLOTS)]
HI, LO = 0, 1


def build(nc, x_d, ctx_d, mask_a_d, mask_b_d, gqa_w, mha_w, out_d):
    B, T, D = x_d.shape
    S, C = ctx_d.shape[1:]
    KC = C // P
    GD = D // H
    KVG = gqa_w[0]["wk"].shape[1] // GD
    R = H // KVG
    INNER = mha_w[0]["Wq"].shape[1]
    MD = INNER // H
    NOC = INNER // P
    HPC = P // MD
    HS = H * S
    HS_PAD = (H - 1) * S + P
    BANK = 512
    NIT = B // STREAMS
    TAIL = max(j for j in range(SLOTS) if ITEMS[j][2]) + 3
    assert T == P and D == P and GD * R * 4 == P and HS <= 3 * BANK

    W_GQA = 16.0
    W_M = 16.0
    W_V = 64.0
    W_P = 4096.0
    MHA_SCALE = float(MD) ** -0.5 / W_M
    Y_SCALE = 1.0 / (W_V * W_V)
    SS_MUL = GD * W_GQA ** 4 / D
    SS_ADD = GD * W_GQA ** 4 * EPS

    def stream(j):
        return ITEMS[j % SLOTS][0]

    def layer(j):
        return ITEMS[j % SLOTS][1]

    def is_gqa(j):
        return layer(j) % 2 == 0

    def following(j):
        return j + (3 if is_gqa(j) else 5)

    def m_place(h):
        return h % HPC * NOC + h // HPC

    def round_of(it, j):
        return it + j // SLOTS - ITEMS[j % SLOTS][2]

    def exists(it, j):
        return not isinstance(it, int) or 0 <= round_of(it, j) < NIT

    HEADS_G = BANK // S
    G_CHUNKS = [(h, min(H, h + HEADS_G)) for h in range(0, H, HEADS_G)]
    V_CHUNKS = [(n, n + BANK) for n in range(0, INNER, BANK)]
    HEADS_O = 6
    TURN = H // 2
    OTURN = 4
    NOT = NOC // OTURN

    gqa_only, mha_only = (1, 0, 1, 0), (0, 1, 0, 1)
    first_only, last_only, each, two = (1, 0, 0, 0), (0, 0, 0, 1), (1, 1, 1, 1), (2, 2, 2, 2)
    EARLY = len(G_CHUNKS) + len(V_CHUNKS) - 1
    n_ctx = (2, EARLY) * 2
    n_o = (1, 2, 1, 2)
    n_ot = (1, NOT, 1, NOT)
    PER_ITEM = {
        "q_raw": gqa_only, "q_hi": gqa_only, "q_lo": gqa_only, "kb": gqa_only,
        "ms": gqa_only, "rstd": gqa_only, "sq": gqa_only, "xb": mha_only,
        "s_raw": each, "s_max": each, "s_sub": each, "p_exp": each, "p_hi": each, "p_lo": each,
        "ctx_raw": n_ctx, "ctx_hi": n_ctx, "ctx_lo": n_ctx,
        "cv_raw": mha_only, "cv_hi": mha_only, "cv_lo": mha_only,
        "turn_raw": (4,) * 4, "turn_hi": two, "turn_lo0": each, "turn_lo1": each,
        "ot_raw": n_ot, "ot_hi": n_ot, "ot_lo": n_ot,
        "o_raw": n_o, "o_rcp": n_o, "o_norm": n_o,
        "y_raw": each, "xg_f32": gqa_only, "xg_hi": gqa_only, "xg_lo": gqa_only,
        "xm_f32": mha_only, "xm_hi": mha_only, "xm_lo": mha_only,
        "x_in": first_only, "ct_raw": first_only, "ct_hi": first_only, "ct_lo": first_only,
        "xr_raw": last_only, "xr": last_only, "out": last_only,
    }

    def at(name, it, j, k):
        per = [PER_ITEM[name][ITEMS[n][1]] for n in range(SLOTS)]
        late = [PER_ITEM[name][ITEMS[n][1]] * ITEMS[n][2] for n in range(SLOTS)]
        it, j = it + j // SLOTS, j % SLOTS
        if isinstance(it, int) and it <= 0:
            return sum(per[:j]) - sum(late[:j]) + k if it == 0 else 0
        if isinstance(it, int) and it == NIT:
            return it * sum(per) - sum(late) + sum(late[:j]) + k
        return it * sum(per) - sum(late) + sum(per[:j]) + k

    def chunks_before(j):
        return [(j + 1, 0)]

    def chunks_after(j):
        return [(j, EARLY), (j + 1, 1)] if is_gqa(j + 1) else [(j + 1, k) for k in range(1, EARLY)]

    def chunk_sem(j, k):
        return ("ctx", k) if k < n_ctx[layer(j)] else ("cv", 0)

    def bank_of(j, k):
        slot = (j if chunk_sem(j, k)[0] == "cv" else j - 1) % SLOTS
        order = [(item % SLOTS, n) for q in range(slot + 1) for item, n in chunks_before(q) + chunks_after(q)]
        return order.index((j % SLOTS, k)) % 2 if (j % SLOTS, k) in order else None

    def bank_before(it, j, k):
        slot = j if chunk_sem(j, k)[0] == "cv" else j - 1
        order = [c for q in range(slot - 5, slot + 1) for c in chunks_before(q) + chunks_after(q)]
        place = order.index((j, k)) - 2
        while place >= 0:
            item = order[place]
            if exists(it, item[0]) and not (isinstance(it, int) and it * SLOTS + item[0] < 0):
                return item
            place -= 2
        return None

    def misc_users(it, j):
        users, o = [], j - 2
        if exists(it, o):
            if layer(o) == LAYERS - 1:
                users += [("xr", o, "xr"), ("y", o, "out")]
            else:
                users.append(("y", following(o), x_sem(following(o), "f32")))
        if is_gqa(j + 1) and exists(it, j + 1):
            users.append(("q", j + 1, "q_lo"))
        if layer(j + 2) == 0 and exists(it, j + 2):
            users += [("x", j + 2, "xg_f32"), ("ct", j + 2, "ct_lo")]
        return users

    def x_sem(j, part):
        return ("xg_" if is_gqa(j) else "xm_") + part

    def misc_before(it, j, kind):
        own = misc_users(it, j)
        n = [u[0] for u in own].index(kind)
        if n:
            return own[n - 1][2], own[n - 1][1]
        for d in range(1, 4):
            if not isinstance(it, int) or it * SLOTS + j - d >= -2:
                if last := misc_users(it, j - d):
                    return last[-1][2], last[-1][1]
        return None

    with ExitStack() as ctx:
        def sb(name, shape, dt):
            return ctx.enter_context(nc.sbuf_tensor(name, shape, dt))

        def ps(name, shape):
            return ctx.enter_context(nc.psum_tensor(name, shape, F32))

        def sem(name):
            return ctx.enter_context(nc.semaphore(name))

        wq_r = [sb(f"wq_r{n}", [P, 2, KVG, 4, R * GD], F16) for n in range(2)]
        wk_r = [sb(f"wk_r{n}", [P, 2, KC, KVG, 4 * R, GD], F16) for n in range(2)]
        wv_g = [sb(f"wv_g{n}", [P, 2, KC, KVG * GD], F16) for n in range(2)]
        wo_g = [sb(f"wo_g{n}", [P, 2, D], F16) for n in range(2)]
        m_w = [sb(f"m_w{n}", [P, 2, H, KC, D], F16) for n in range(2)]
        wv_m = [sb(f"wv_m{n}", [P, 2, KC, INNER], F16) for n in range(2)]
        wo_m = [sb(f"wo_m{n}", [P, 2, NOC, D], F16) for n in range(2)]
        norm_w = sb("norm_w", [P, 2], F32)
        bo = sb("bo", [P, 2], F32)
        arena = sb("arena", [P, ARENA], F32)
        taken = [0]

        def in_arena(width, dt):
            words = width if dt == F32 else (width + 1) // 2
            view = arena[:, taken[0]:taken[0] + words]
            taken[0] += words
            assert taken[0] <= ARENA
            return view if dt == F32 else view.bitcast(dt)[:, 0:width]

        st_wq = in_arena(INNER, F32)
        st_wk = in_arena(KC * INNER, F32).rearrange("p (k n) -> p k n", k=KC)
        st_wv = in_arena(KC * INNER, F32).rearrange("p (k n) -> p k n", k=KC)
        st_wo = in_arena(NOC * D, F32).rearrange("p (k n) -> p k n", k=NOC)
        wq_t = in_arena(NOC * D, F32).rearrange("p (a b) -> p a b", a=NOC)
        wk_t = in_arena(NOC * C, F32).rearrange("p (a b) -> p a b", a=NOC)
        taken[0] = 0
        g_s = in_arena(2 * HS, F16).rearrange("p (a n) -> p a n", a=2)
        k_bd = in_arena(HS, F16).rearrange("p (g r s) -> p g r s", g=KVG, s=S)
        probs = in_arena(HS, F32)
        shifted = in_arena(HS, F32).rearrange("p (h s) -> p h s", s=S)
        p_t = in_arena(2 * H * T, F16).rearrange("p (a h t) -> p a h t", a=2, t=T)
        o_n = in_arena(NOC * P, F32).rearrange("p (c d) -> p c d", d=P)
        o_t = in_arena(2 * NOC * T, F16).rearrange("p (a c t) -> p a c t", a=2, t=T)
        st_gq = sb("st_gq", [P, 2, D], F32)
        st_gk = sb("st_gk", [P, 2, KC, KVG * GD], F32)
        st_gv = sb("st_gv", [P, 2, KC, KVG * GD], F32)
        st_go = sb("st_go", [P, 2, D], F32)
        ident = sb("ident", [P, P], F32)
        ident_h = sb("ident_h", [P, P], F16)
        log_w = sb("log_w", [P, 1], F32)
        ones = sb("ones", [P, 1], F32)
        minus_half = sb("minus_half", [P, 1], F32)
        part_i = sb("part_i", [P, 1], I32)
        part_f = sb("part_f", [P, 2], F32)
        head_i = sb("head_i", [P, 1], I32)
        head_mask = sb("head_mask", [P, R], F32)
        key_i = sb("key_i", [P, S], I32)
        key_f = sb("key_f", [P, S], F32)
        tok_i = sb("tok_i", [6, 4, 2], I32)
        tok_f = sb("tok_f", [6, 4, 2], F32)
        tok_w = sb("tok_w", [6, 4, 2], F32)
        hit = sb("hit", [6, 4, 2, S], F32)
        hit_any = sb("hit_any", [6, 4, S], F32)
        row_sel = sb("row_sel", [6, 8], F32)
        mask_r = sb("mask_r", [6, 8, P], F32)
        mask_p = sb("mask_p", [6, 3, P], BF16)
        bias_l = sb("bias_l", [P, P], BF16)
        bias_r = [sb(f"bias_r{n}", [P, H, S], BF16) for n in range(2)]
        x_nat = [sb(f"x_nat{n}", [P, D], F32) for n in range(STREAMS)]
        ctx_nat = [sb(f"ctx_nat{n}", [S, C], F32) for n in range(STREAMS)]
        ctx_t = [sb(f"ctx_t{n}", [P, 2, KC, S], F16) for n in range(STREAMS)]
        x_f = [sb(f"x_f{n}", [P, T], F32) for n in range(STREAMS)]
        x_b = [sb(f"x_b{n}", [P, T], F32) for n in range(STREAMS)]
        x_s = [sb(f"x_s{n}", [P, 2, T], F16) for n in range(STREAMS)]
        x_sq = [sb(f"x_sq{n}", [P, T], F32) for n in range(STREAMS)]
        y_out = [sb(f"y_out{n}", [P, D], F32) for n in range(STREAMS)]
        v_gqa = [sb(f"v_gqa{n}", [P, 2, KVG, GD + 1], F16) for n in range(2)]
        v_mha = [sb(f"v_mha{n}", [P, 2, H, MD + 1], F16) for n in range(2)]
        p_s = [sb(f"p_s{n}", [P, 2, HS_PAD], F16) for n in range(2)]
        ms = sb("ms", [P, 2], F32)
        rstd = sb("rstd", [P, 2], F32)
        k_rep = sb("k_rep", [P, KVG, S], F16)
        q_rep = sb("q_rep", [P, KVG, T], F16)
        row_max = sb("row_max", [P, H], F32)
        den_r = sb("den_r", [P, 3 * HEADS_O], F32)
        x_res = sb("x_res", [P, D], F32)

        so = ps("so", [P, 3, BANK])
        ring_c = ps("ring_c", [P, 2, BANK])
        ring_t = ps("ring_t", [P, 2, BANK])
        misc = ps("misc", [P, BANK])
        so_flat = so[:, :, :].rearrange("p b n -> p (b n)")
        s_view = so_flat[:, 0:HS].rearrange("p (h s) -> p h s", s=S)
        ring_th = [ring_t[:, n, :].bitcast(F16) for n in range(2)]
        SS_COL = HS + 64

        sems = {name: sem(name) for name in PER_ITEM}
        load_x = [sem(f"load_x{n}") for n in range(STREAMS)]
        load_c = [sem(f"load_c{n}") for n in range(STREAMS)]
        stored = [sem(f"stored{n}") for n in range(STREAMS)]
        load_small = sem("load_small")
        load_qk = sem("load_qk")
        load_vo = sem("load_vo")
        vo_free = sem("vo_free")
        consts_pool = sem("consts_pool")
        pool_step = sem("pool_step")
        dve_step = sem("dve_step")
        act_split = sem("act_split")
        dve_ready = sem("dve_ready")
        prep_raw = sem("prep_raw")
        prep_hi = sem("prep_hi")
        prep_free = sem("prep_free")

        NTQ = NOC // 4
        NTK = NOC * KC // 4
        NMM = H * KC // 4
        PREP = NTQ + NTK + NMM

        block = ctx.enter_context(nc.Block())

        @block.sync
        def _(sp):
            n_small = 0
            for row, d in ((0, mask_a_d), (3, mask_b_d)):
                sp.dma_start(mask_r[row:row + 3, 0, :],
                             d.rearrange("(a t) -> a t", a=1).to_broadcast([3, T])).then_inc(load_small, 16)
                n_small += 1
            for n in range(2):
                for row, d in ((0, mha_w[n]["tok_a"]), (3, mha_w[n]["tok_b"])):
                    sp.dma_start(tok_i[row:row + 3, 2 * n, :],
                                 d.rearrange("(a t) -> a t", a=1).to_broadcast([3, 2])).then_inc(load_small, 16)
                sp.dma_start(tok_i[0:6, 2 * n + 1, :],
                             mha_w[n]["tok_b"].rearrange("(a t) -> a t", a=1).to_broadcast([6, 2])).then_inc(load_small, 16)
                sp.dma_start(norm_w[:, n:n + 1], gqa_w[n]["norm_w"].rearrange("(p a) -> p a", a=1)).then_inc(load_small, 16)
                sp.dma_start(bo[:, n:n + 1], mha_w[n]["bo"].rearrange("(p a) -> p a", a=1)).then_inc(load_small, 16)
                sp.dma_start(st_gq[:, n, :], gqa_w[n]["wq"]).then_inc(load_small, 16)
                sp.dma_start(st_gk[:, n, :, :], gqa_w[n]["wk"].rearrange("(k p) n -> p k n", p=P)).then_inc(load_small, 16)
                sp.dma_start(st_gv[:, n, :, :], gqa_w[n]["wv"].rearrange("(k p) n -> p k n", p=P)).then_inc(load_small, 16)
                sp.dma_start(st_go[:, n, :], gqa_w[n]["wo"]).then_inc(load_small, 16)
                n_small += 9
            assert n_small == SMALL_LOADS
            for st in range(STREAMS):
                sp.dma_start(x_nat[st][:, :], x_d[st, :, :]).then_inc(load_x[st], 16)
                sp.dma_start(ctx_nat[st][:, :], ctx_d[st, :, :]).then_inc(load_c[st], 16)
            for n in range(2):
                if n:
                    sp.wait_ge(prep_free, n * PREP)
                sp.dma_start(st_wq, mha_w[n]["Wq"]).then_inc(load_qk, 16)
                sp.dma_start(st_wk, mha_w[n]["Wk"].rearrange("(k p) n -> p k n", p=P)).then_inc(load_qk, 16)
                if n:
                    sp.wait_ge(vo_free, 2 * n)
                sp.dma_start(st_wv, mha_w[n]["Wv"].rearrange("(k p) n -> p k n", p=P)).then_inc(load_vo, 16)
                sp.dma_start(st_wo, mha_w[n]["Wo"].rearrange("(k p) n -> p k n", p=P)).then_inc(load_vo, 16)

            def slot(it, j):
                c, o = j + 2, j - 2
                if layer(c) == 0 and exists(it, c) and exists(it + 1, c):
                    st, n = stream(c), round_of(it, c) + 1
                    sp.wait_ge(sems["x_in"], at("x_in", it, c, 1))
                    sp.dma_start(x_nat[st][:, :], x_d[n * STREAMS + st, :, :]).then_inc(load_x[st], 16)
                    sp.wait_ge(sems["ct_raw"], at("ct_raw", it, c, 1))
                    sp.dma_start(ctx_nat[st][:, :], ctx_d[n * STREAMS + st, :, :]).then_inc(load_c[st], 16)
                if layer(o) == LAYERS - 1 and exists(it, o):
                    sp.wait_ge(sems["out"], at("out", it, o, 1))
                    sp.dma_start(out_d[round_of(it, o) * STREAMS + stream(o), :, :], y_out[stream(o)][:, :]).then_inc(stored[stream(o)], 16)

            for j in range(-2, SLOTS):
                slot(0, j)
            with sp.Fori(1, NIT - 2) as it:
                for j in range(SLOTS):
                    slot(it, j)
            for j in range(2 * SLOTS):
                slot(NIT - 2 + j // SLOTS, j % SLOTS)
            for j in range(TAIL):
                slot(NIT, j)
            for st in range(STREAMS):
                sp.wait_ge(stored[st], 16 * (NIT + 1))

        @block.gpsimd
        def _(pool):
            pool.memset(ident[:, :], 0.0).then_inc(pool_step, 1)
            pool.memset(ones[:, :], 1.0).then_inc(consts_pool, 1)
            pool.memset(minus_half[:, :], -0.5).then_inc(consts_pool, 1)
            pool.iota(part_i[:, :], pattern=[[0, 1]], base=0, channel_multiplier=1).then_inc(consts_pool, 1)
            pool.iota(key_i[:, :], pattern=[[1, S]], base=0, channel_multiplier=0).then_inc(consts_pool, 1)
            pool.memset(bias_l[:, :], 0.0).then_inc(consts_pool, 1)
            for n in range(2):
                pool.memset(bias_r[n][:, :, :], 0.0).then_inc(consts_pool, 1)
                pool.memset(p_s[n][:, :, HS:HS_PAD], 0.0).then_inc(consts_pool, 1)
            pool.memset(log_w[:, :], float(np.log(W_P))).then_inc(consts_pool, 1)
            for n in range(2):
                pool.memset(v_gqa[n][:, :, :, :], 0.0).then_inc(pool_step, 1)
                pool.memset(v_mha[n][:, :, :, :], 0.0).then_inc(pool_step, 1)
            for n in range(STREAMS):
                pool.memset(y_out[n][:, :], 0.0).then_inc(stored[n], 16)
            pool.wait_ge(pool_step, 5)
            pool.affine_select(out=ident[:, :], in_=ident[:, :], compare_op=ALU.not_equal, fill=1.0, base=0,
                               pattern=[[-1, P]], channel_multiplier=1).then_inc(pool_step, 1)
            for n in range(2):
                pool.memset(v_gqa[n][0:S, HI, :, GD:GD + 1], 1.0).then_inc(consts_pool, 1)
                pool.memset(v_mha[n][0:S, HI, :, MD:MD + 1], 1.0).then_inc(consts_pool, 1)
            pool.wait_ge(pool_step, 6)
            pool.tensor_copy(ident_h[:, :], ident[:, :]).then_inc(consts_pool, 1)
            pool.wait_ge(load_small, 16 * SMALL_LOADS)

            def x_parts(it, j):
                st = stream(j)
                pool.wait_ge(sems[x_sem(j, "f32")], at(x_sem(j, "f32"), it, j, 1))
                if is_gqa(j):
                    pool.tensor_tensor(x_sq[st][:, :], x_f[st][:, :], x_f[st][:, :], ALU.mult).then_inc(sems["sq"], 1)
                else:
                    n = layer(j) // 2
                    pool.tensor_tensor(x_b[st][:, :], x_f[st][:, :], bo[:, n:n + 1].to_broadcast([P, T]), ALU.add).then_inc(sems["xb"], 1)
                pool.tensor_copy(x_s[st][:, HI, :], x_f[st][:, :]).then_inc(sems[x_sem(j, "hi")], 1)
                pool.wait_ge(sems[x_sem(j, "hi")], at(x_sem(j, "hi"), it, j, 1))
                pool.tensor_tensor(x_s[st][:, LO, :], x_f[st][:, :], x_s[st][:, HI, :], ALU.subtract).then_inc(sems[x_sem(j, "lo")], 1)

            def slot(it, j):
                par, o = j % 2, j - 2
                if is_gqa(j) and exists(it, j):
                    r = j // 2 % 2
                    pool.wait_ge(sems["ms"], at("ms", it, j, 1))
                    pool.tensor_tensor(rstd[:, r:r + 1], ms[:, r:r + 1], minus_half[:, :], ALU.pow).then_inc(sems["rstd"], 1)
                if exists(it, o) and layer(o) < LAYERS - 1:
                    x_parts(it, following(o))
                if exists(it, j):
                    pool.wait_ge(sems["p_hi"], at("p_hi", it, j, 1))
                    pool.tensor_tensor(p_s[par][:, LO, 0:HS], probs, p_s[par][:, HI, 0:HS], ALU.subtract).then_inc(sems["p_lo"], 1)
                if layer(j + 2) == 0 and exists(it, j + 2):
                    x_parts(it, j + 2)

            for j in range(-2, SLOTS):
                slot(0, j)
            with pool.Fori(1, NIT - 1) as it:
                for j in range(SLOTS):
                    slot(it, j)
            for j in range(SLOTS):
                slot(NIT - 1, j)
            for j in range(TAIL):
                slot(NIT, j)

        @block.scalar
        def _(act):
            def high(out, in_, scale):
                return act.activation(out, in_, ACT.Copy, scale=scale)

            act.wait_ge(load_small, 16 * SMALL_LOADS)
            act.wait_ge(dve_ready, 1)
            for n in range(2):
                high(wq_r[n][:, HI], st_gq[:, n, :].rearrange("p (g a e) -> p g a e", g=KVG, a=1).to_broadcast([P, KVG, 4, R * GD]), W_GQA).then_inc(act_split, 1)
                for kc in range(KC):
                    high(wk_r[n][:, HI, kc], st_gk[:, n, kc, :].rearrange("p (g a e) -> p g a e", g=KVG, a=1).to_broadcast([P, KVG, 4 * R, GD]), W_GQA).then_inc(act_split, 1)
                high(wv_g[n][:, HI], st_gv[:, n, :, :], W_V).then_inc(act_split, 1)
                high(wo_g[n][:, HI], st_go[:, n, :], W_V).then_inc(act_split, 1)
            for n in range(2):
                for c in range(NMM):
                    k = n * PREP + NTQ + NTK + c
                    act.wait_ge(prep_raw, k + 1)
                    high(m_w[n][:, HI].rearrange("p h k c -> p (h k c)")[:, c * BANK:(c + 1) * BANK], ring_t[:, k % 2, :], W_M).then_inc(prep_hi, 1)
                act.wait_ge(load_vo, 32 * (n + 1))
                high(wv_m[n][:, HI], st_wv, W_V).then_inc(act_split, 1)
                high(wo_m[n][:, HI], st_wo, W_V).then_inc(act_split, 1)

            def turn_context(it, j):
                act.wait_ge(sems["ct_raw"], at("ct_raw", it, j, 1))
                high(ctx_t[stream(j)][:, HI], misc[:, 0:KC * S].rearrange("p (k s) -> p k s", s=S), 1.0).then_inc(sems["ct_hi"], 1)

            def context_chunk(it, j, k):
                st = stream(j)
                b = bank_of(j, k)
                fam, i = chunk_sem(j, k)
                act.wait_ge(sems[fam + "_raw"], at(fam + "_raw", it, j, i + 1))
                if is_gqa(j) and k == 0:
                    if not (isinstance(it, int) and at("kb", it, j, 0) == 0):
                        act.wait_ge(sems["kb"], at("kb", it, j, 0))
                    ins = high(k_rep[:, :, :], ring_c[:, b, 0:KVG * S].rearrange("p (g s) -> p g s", s=S), 1.0)
                elif is_gqa(j):
                    ins = high(v_gqa[j // 2 % 2][0:S, HI, :, 0:GD], ring_c[0:S, b, 0:KVG * GD].rearrange("p (g d) -> p g d", d=GD), 1.0)
                elif k < len(G_CHUNKS):
                    h0, h1 = G_CHUNKS[k]
                    ins = high(g_s[:, HI, h0 * S:h1 * S], ring_c[:, b, 0:(h1 - h0) * S], 1.0)
                else:
                    n0, n1 = V_CHUNKS[k - len(G_CHUNKS)]
                    ins = high(v_mha[j // 2 % 2][0:S, HI, n0 // MD:n1 // MD, 0:MD], ring_c[0:S, b, :].rearrange("p (h d) -> p h d", d=MD), 1.0)
                ins.then_inc(sems[fam + "_hi"], 1)

            def turned_probs(it, j, k):
                x, half = divmod(k, 2)
                act.wait_ge(sems["turn_raw"], at("turn_raw", it, j, k + 1))
                act.activation(p_t[:, x, half * TURN:(half + 1) * TURN, :], ring_th[half].rearrange("p (h t) -> p h t", t=T),
                               ACT.Copy).then_inc(sems["turn_lo0" if x else "turn_hi"], 1)

            def turned_o(it, j, k):
                n = 1 if is_gqa(j) else OTURN
                act.wait_ge(sems["ot_raw"], at("ot_raw", it, j, k + 1))
                high(o_t[:, HI, k * OTURN:k * OTURN + n, :], ring_t[:, k, 0:n * T].rearrange("p (h t) -> p h t", t=T), 1.0).then_inc(sems["ot_hi"], 1)

            def slot(it, j):
                c, p, o, par = j + 1, j - 1, j - 2, j % 2
                if exists(it, o) and layer(o) == LAYERS - 1:
                    act.wait_ge(sems["xr_raw"], at("xr_raw", it, o, 1))
                    high(x_res[:, :], misc[:, 0:D], 1.0).then_inc(sems["xr"], 1)
                if exists(it, p):
                    turned_probs(it, p, 0)
                    turned_probs(it, p, 1)
                for item, k in chunks_before(j):
                    if exists(it, item):
                        context_chunk(it, item, k)
                if exists(it, p):
                    turned_probs(it, p, 2)
                if exists(it, j):
                    r = j // 2 % 2
                    act.wait_ge(sems["s_sub"], at("s_sub", it, j, 1))
                    if is_gqa(j):
                        act.wait_ge(sems["rstd"], at("rstd", it, j, 1))
                    if not (isinstance(it, int) and at("p_lo", it, j, 0) == 0):
                        act.wait_ge(sems["p_lo"], at("p_lo", it, j, 0))
                    act.activation(probs, shifted.rearrange("p h s -> p (h s)"), ACT.Exp, bias=log_w[:, :],
                                   scale=rstd[:, r:r + 1] if is_gqa(j) else MHA_SCALE).then_inc(sems["p_exp"], 1)
                    act.wait_ge(sems["p_exp"], at("p_exp", it, j, 1))
                    high(p_s[par][:, HI, 0:HS], probs, 1.0).then_inc(sems["p_hi"], 1)
                after = [a for a in chunks_after(j) if exists(it, a[0])]
                if is_gqa(c):
                    if exists(it, c):
                        act.wait_ge(sems["q_raw"], at("q_raw", it, c, 1))
                        high(q_rep[:, :, :], misc[:, :].rearrange("p (g t) -> p g t", t=T), 1.0).then_inc(sems["q_hi"], 1)
                    if exists(it, p):
                        turned_o(it, p, 0)
                    for item, k in after:
                        context_chunk(it, item, k)
                    return
                for item, k in after[:2]:
                    context_chunk(it, item, k)
                if exists(it, p):
                    for k in range(NOT):
                        turned_o(it, p, k)
                for item, k in after[2:]:
                    context_chunk(it, item, k)
                if layer(j + 2) == 0 and exists(it, j + 2):
                    turn_context(it, j + 2)

            for j in range(-2, SLOTS):
                slot(0, j)
            with act.Fori(1, NIT - 1) as it:
                for j in range(SLOTS):
                    slot(it, j)
            for j in range(SLOTS):
                slot(NIT - 1, j)
            for j in range(TAIL):
                slot(NIT, j)

        @block.vector
        def _(dve):
            def low(out, in_, scale, hi):
                return dve.scalar_tensor_tensor(out=out, in0=in_, scalar=scale, in1=hi, op0=ALU.mult, op1=ALU.subtract)

            steps = [0]

            def step(ins):
                steps[0] += 1
                ins.then_inc(dve_step, 1)
                dve.wait_ge(dve_step, steps[0])

            dve.wait_ge(consts_pool, CONSTS)
            dve.wait_ge(load_small, 16 * SMALL_LOADS)
            for n in range(2):
                step(dve.tensor_scalar(st_gq[:, n, :], st_gq[:, n, :], norm_w[:, n:n + 1], None, ALU.mult))
            step(dve.tensor_copy(part_f[:, 0:1], part_i[:, :]))
            dve.tensor_copy(key_f[:, :], key_i[:, :]).then_inc(dve_ready, 1)
            step(dve.tensor_scalar(head_i[:, :], part_i[:, :], int(np.log2(GD)), R - 1, ALU.logical_shift_right, ALU.bitwise_and))
            step(dve.tensor_copy(part_f[:, 1:2], head_i[:, :]))
            for r in range(R):
                step(dve.tensor_scalar(head_mask[:, r:r + 1], part_f[:, 1:2], float(r), None, ALU.is_equal))
            for k in range(3):
                step(dve.tensor_scalar(row_sel[:, k:k + 1], part_f[0:6, 0:1], float(k), None, ALU.is_equal))
                step(dve.tensor_scalar(row_sel[:, 4:5], part_f[0:6, 0:1], float(k + 3), None, ALU.is_equal))
                step(dve.tensor_tensor(row_sel[:, k:k + 1], row_sel[:, k:k + 1], row_sel[:, 4:5], ALU.add))
            step(dve.tensor_scalar(row_sel[:, 3:4], part_f[0:6, 0:1], 3.0, None, ALU.is_lt))
            tok_flat = tok_f[:, :, :].rearrange("p a b -> p (a b)")
            wrap_flat = tok_w[:, :, :].rearrange("p a b -> p (a b)")
            step(dve.tensor_copy(tok_flat, tok_i[:, :, :].rearrange("p a b -> p (a b)")))
            step(dve.tensor_scalar(wrap_flat, tok_flat, 0.0, float(S), ALU.is_lt, ALU.mult))
            step(dve.tensor_tensor(tok_flat, tok_flat, wrap_flat, ALU.add))
            for a in range(4):
                for b in range(2):
                    step(dve.tensor_scalar(hit[:, a, b, :], key_f[0:6, :], tok_f[:, a, b:b + 1], None, ALU.is_equal))
                step(dve.tensor_tensor(hit_any[:, a, :], hit[:, a, 0, :], hit[:, a, 1, :], ALU.max))
            for n in range(2):
                own, over = hit_any[:, 2 * n, :], hit_any[:, 2 * n + 1, :]
                step(dve.tensor_scalar(over, over, row_sel[:, 3:4], -1.0, ALU.mult, ALU.mult))
                step(dve.tensor_scalar(over, over, 1.0, None, ALU.add))
                step(dve.tensor_tensor(own, own, over, ALU.mult))
                step(dve.tensor_copy(bias_r[n][0:6, :, :], own.unsqueeze(1).to_broadcast([6, H, S])))
            m = [mask_r[:, k, :] for k in range(8)]
            step(dve.tensor_scalar(m[1], m[0], -1.0, 1.0, ALU.mult, ALU.add))
            step(dve.tensor_scalar(m[2], m[1], -SUPPRESS, 1.0 / MHA_SCALE, ALU.mult, ALU.mult))
            step(dve.tensor_copy(mask_p[:, 0, :], m[2]))
            step(dve.tensor_tensor(m[3], m[2], mask_p[:, 0, :], ALU.subtract))
            step(dve.tensor_copy(mask_p[:, 1, :], m[3]))
            step(dve.tensor_tensor(m[4], m[3], mask_p[:, 1, :], ALU.subtract))
            step(dve.tensor_copy(mask_p[:, 2, :], m[4]))
            step(dve.tensor_scalar(m[5], mask_p[:, 0, :], row_sel[:, 0:1], None, ALU.mult))
            step(dve.scalar_tensor_tensor(out=m[6], in0=mask_p[:, 1, :], scalar=row_sel[:, 1:2], in1=m[5], op0=ALU.mult, op1=ALU.add))
            step(dve.scalar_tensor_tensor(out=bias_l[0:6, :], in0=mask_p[:, 2, :], scalar=row_sel[:, 2:3], in1=m[6], op0=ALU.mult, op1=ALU.add))

            assert steps[0] == DVE_STEPS, steps[0]

            NSPLIT = 3 + KC
            for n in range(2):
                dve.wait_ge(act_split, NSPLIT * (n + 1))
                for g in range(KVG):
                    low(wq_r[n][:, LO, g], st_gq[:, n, g * R * GD:(g + 1) * R * GD].unsqueeze(1).to_broadcast([P, 4, R * GD]), W_GQA, wq_r[n][:, HI, g]).then_inc(dve_ready, 1)
                for kc in range(KC):
                    for g in range(KVG):
                        low(wk_r[n][:, LO, kc, g], st_gk[:, n, kc, g * GD:(g + 1) * GD].unsqueeze(1).to_broadcast([P, 4 * R, GD]), W_GQA, wk_r[n][:, HI, kc, g]).then_inc(dve_ready, 1)
                low(wv_g[n][:, LO], st_gv[:, n, :, :], W_V, wv_g[n][:, HI]).then_inc(dve_ready, 1)
                low(wo_g[n][:, LO], st_go[:, n, :], W_V, wo_g[n][:, HI]).then_inc(dve_ready, 1)
            for n in range(2):
                for c in range(NTQ + NTK):
                    k = n * PREP + c
                    dve.wait_ge(prep_raw, k + 1)
                    dst = (wq_t if c < NTQ else wk_t).rearrange("p a b -> p (a b)")
                    o = (c if c < NTQ else c - NTQ) * BANK
                    dve.tensor_copy(dst[:, o:o + BANK], ring_t[:, k % 2, :]).then_inc(prep_free, 1)
                for c in range(NMM):
                    k = n * PREP + NTQ + NTK + c
                    dve.wait_ge(prep_hi, n * NMM + c + 1)
                    part = slice(c * BANK, (c + 1) * BANK)
                    low(m_w[n][:, LO].rearrange("p h k c -> p (h k c)")[:, part], ring_t[:, k % 2, :], W_M,
                        m_w[n][:, HI].rearrange("p h k c -> p (h k c)")[:, part]).then_inc(prep_free, 1)
                dve.wait_ge(act_split, 2 * NSPLIT + 2 * (n + 1))
                low(wv_m[n][:, LO], st_wv, W_V, wv_m[n][:, HI]).then_inc(vo_free, 1)
                low(wo_m[n][:, LO], st_wo, W_V, wo_m[n][:, HI]).then_inc(vo_free, 1)

            def turn_context(it, j):
                st = stream(j)
                dve.wait_ge(sems["ct_hi"], at("ct_hi", it, j, 1))
                low(ctx_t[st][:, LO], misc[:, 0:KC * S].rearrange("p (k s) -> p k s", s=S), 1.0, ctx_t[st][:, HI]).then_inc(sems["ct_lo"], 1)

            def context_chunk(it, j, k):
                st = stream(j)
                b = bank_of(j, k)
                fam, i = chunk_sem(j, k)
                dve.wait_ge(sems[fam + "_hi"], at(fam + "_hi", it, j, i + 1))
                if is_gqa(j) and k == 0:
                    raw = ring_c[:, b, 0:KVG * S].rearrange("p (g s) -> p g s", s=S)
                    low(k_rep[32:64], raw[32:64], 1.0, k_rep[32:64])
                    low(k_rep[96:128], raw[96:128], 1.0, k_rep[96:128]).then_inc(sems["ctx_lo"], 1)
                    dve.wait_ge(sems["ctx_lo"], at("ctx_lo", it, j, 1))
                    for r in range(R):
                        ins = dve.tensor_scalar(k_bd[:, :, r, :], k_rep[:, :, :], head_mask[:, r:r + 1], None, ALU.mult)
                    ins.then_inc(sems["kb"], 1)
                    return
                if is_gqa(j):
                    v = v_gqa[j // 2 % 2]
                    ins = low(v[0:S, LO, :, 0:GD], ring_c[0:S, b, 0:KVG * GD].rearrange("p (g d) -> p g d", d=GD), 1.0, v[0:S, HI, :, 0:GD])
                elif k < len(G_CHUNKS):
                    h0, h1 = G_CHUNKS[k]
                    ins = low(g_s[:, LO, h0 * S:h1 * S], ring_c[:, b, 0:(h1 - h0) * S], 1.0, g_s[:, HI, h0 * S:h1 * S])
                else:
                    n0, n1 = V_CHUNKS[k - len(G_CHUNKS)]
                    v, hs = v_mha[j // 2 % 2], slice(n0 // MD, n1 // MD)
                    ins = low(v[0:S, LO, hs, 0:MD], ring_c[0:S, b, :].rearrange("p (h d) -> p h d", d=MD), 1.0, v[0:S, HI, hs, 0:MD])
                ins.then_inc(sems[fam + "_lo"], 1)

            def turned_probs(it, j):
                dve.wait_ge(sems["turn_raw"], at("turn_raw", it, j, 4))
                dve.tensor_copy(p_t[:, LO, TURN:H, :], ring_th[1].rearrange("p (h t) -> p h t", t=T)).then_inc(sems["turn_lo1"], 1)

            def turned_o(it, j, k):
                n = 1 if is_gqa(j) else OTURN
                cs = slice(k * OTURN, k * OTURN + n)
                dve.wait_ge(sems["ot_hi"], at("ot_hi", it, j, k + 1))
                low(o_t[:, LO, cs, :], ring_t[:, k, 0:n * T].rearrange("p (h t) -> p h t", t=T), 1.0, o_t[:, HI, cs, :]).then_inc(sems["ot_lo"], 1)

            def normalise(it, j, k):
                dve.wait_ge(sems["o_raw"], at("o_raw", it, j, k + 1))
                if is_gqa(j):
                    o = so_flat[:, 0:H * (GD + 1)].rearrange("p (h d) -> p h d", d=GD + 1)
                    r = den_r[:, 0:H].unsqueeze(2)
                    dst, width = o_n[:, 0, :].rearrange("p (h d) -> p h d", d=GD), [P, H, GD]
                    num, den = o[:, :, 0:GD], o[:, :, GD:GD + 1]
                else:
                    b0, nb, nh = ((0, 2, HEADS_O), (2, 1, H - 2 * HEADS_O))[k]
                    o = so[:, b0:b0 + nb, 0:nh * (MD + 1)].rearrange("p b (h d) -> p b h d", d=MD + 1)
                    h0 = b0 * HEADS_O
                    r = den_r[:, h0:h0 + nb * nh].rearrange("p (b h a) -> p b h a", h=nh, a=1)
                    dst = o_n.rearrange("p c (a d) -> p (c a d)", d=MD)[:, h0 * MD:(h0 + nb * nh) * MD].rearrange("p (b h d) -> p b h d", h=nh, d=MD)
                    num, den, width = o[:, :, :, 0:MD], o[:, :, :, MD:MD + 1], [P, nb, nh, MD]
                dve.reciprocal(r, den).then_inc(sems["o_rcp"], 1)
                dve.wait_ge(sems["o_rcp"], at("o_rcp", it, j, k + 1))
                dve.tensor_tensor(dst, num, r.to_broadcast(width), ALU.mult).then_inc(sems["o_norm"], 1)

            def first_x(it, j):
                dve.wait_ge(sems["x_in"], at("x_in", it, j, 1))
                dve.tensor_copy(x_f[stream(j)][:, :], misc[:, 0:T]).then_inc(sems["xg_f32"], 1)

            def finish(it, p):
                st = stream(p)
                dve.wait_ge(sems["y_raw"], at("y_raw", it, p, 1))
                if layer(p) == LAYERS - 1:
                    dve.wait_ge(sems["xr"], at("xr", it, p, 1))
                    dve.wait_ge(stored[st], 16 * (round_of(it, p) + 1))
                    dve.scalar_tensor_tensor(out=y_out[st][:, :], in0=misc[:, 0:D], scalar=Y_SCALE, in1=x_res[:, :],
                                             op0=ALU.mult, op1=ALU.add).then_inc(sems["out"], 1)
                    return
                base = x_f[st]
                if not is_gqa(p):
                    dve.wait_ge(sems["xb"], at("xb", it, p, 1))
                    base = x_b[st]
                dve.scalar_tensor_tensor(out=x_f[st][:, :], in0=misc[:, 0:T], scalar=Y_SCALE, in1=base[:, :],
                                         op0=ALU.mult, op1=ALU.add).then_inc(sems[x_sem(following(p), "f32")], 1)

            def slot(it, j):
                c, p, o = j + 1, j - 1, j - 2
                if exists(it, j):
                    r = j // 2 % 2
                    dve.wait_ge(sems["s_raw"], at("s_raw", it, j, 1))
                    if is_gqa(j):
                        dve.tensor_scalar(ms[:, r:r + 1], so_flat[:, SS_COL:SS_COL + 1], SS_MUL, SS_ADD, ALU.mult, ALU.add).then_inc(sems["ms"], 1)
                    dve.tensor_reduce(row_max[:, :], s_view, AX_X, ALU.max).then_inc(sems["s_max"], 1)
                    dve.wait_ge(sems["s_max"], at("s_max", it, j, 1))
                    if not (isinstance(it, int) and at("p_exp", it, j, 0) == 0):
                        dve.wait_ge(sems["p_exp"], at("p_exp", it, j, 0))
                    dve.tensor_tensor(shifted, s_view, row_max[:, :].unsqueeze(2).to_broadcast([P, H, S]), ALU.subtract).then_inc(sems["s_sub"], 1)
                if exists(it, p):
                    turned_probs(it, p)
                if exists(it, o):
                    finish(it, o)
                for item, k in chunks_before(j):
                    if exists(it, item):
                        context_chunk(it, item, k)
                if exists(it, p):
                    for k in range(PER_ITEM["o_raw"][layer(p)]):
                        normalise(it, p, k)
                after = [a for a in chunks_after(j) if exists(it, a[0])]
                if is_gqa(c):
                    if exists(it, c):
                        dve.wait_ge(sems["q_hi"], at("q_hi", it, c, 1))
                        low(q_rep[64:128], misc[64:128, :].rearrange("p (g t) -> p g t", t=T), 1.0, q_rep[64:128]).then_inc(sems["q_lo"], 1)
                    if exists(it, p):
                        turned_o(it, p, 0)
                    for item, k in after:
                        context_chunk(it, item, k)
                    return
                first = layer(j + 2) == 0 and exists(it, j + 2)
                for item, k in after[:2]:
                    context_chunk(it, item, k)
                if first:
                    first_x(it, j + 2)
                if exists(it, p):
                    for k in range(NOT):
                        turned_o(it, p, k)
                for item, k in after[2:]:
                    context_chunk(it, item, k)
                if first:
                    turn_context(it, j + 2)

            for j in range(-2, SLOTS):
                slot(0, j)
            with dve.Fori(1, NIT - 1) as it:
                for j in range(SLOTS):
                    slot(it, j)
            for j in range(SLOTS):
                slot(NIT - 1, j)
            for j in range(TAIL):
                slot(NIT, j)

        @block.tensor
        def _(pe):
            def split_product(out, terms):
                passes = [(a[x], b[y]) for a, b in terms for x, y in ((HI, HI), (HI, LO), (LO, HI))]
                for n, (a, b) in enumerate(passes):
                    ins = pe.matmul(out, a, b, start=(n == 0), stop=(n == len(passes) - 1))
                return ins

            def hl(f):
                return f(HI), f(LO)

            pe.wait_ge(consts_pool, CONSTS)
            for n in range(2):
                pe.wait_ge(load_qk, 32 * (n + 1))
                k = n * PREP
                blocks = [(st_wq[:, c * P:(c + 1) * P]) for c in range(NOC)]
                blocks += [(st_wk[:, kc, c * P:(c + 1) * P]) for c in range(NOC) for kc in range(KC)]
                for q in range(0, len(blocks), 4):
                    if k >= 2:
                        pe.wait_ge(prep_free, k - 1)
                    for m in range(4):
                        ins = pe.transpose(ring_t[:, k % 2, m * P:(m + 1) * P], blocks[q + m], ident[:, :])
                    ins.then_inc(prep_raw, 1)
                    k += 1
                pe.wait_ge(prep_free, n * PREP + NTQ + NTK)
                for q in range(0, H * KC, 4):
                    pe.wait_ge(prep_free, k - 1)
                    for m in range(4):
                        place, kc = divmod(q + m, KC)
                        r, pair = place // NOC * MD, place % NOC
                        ins = pe.matmul(ring_t[:, k % 2, m * P:(m + 1) * P], wk_t[r:r + MD, pair, kc * P:(kc + 1) * P],
                                        wq_t[r:r + MD, pair, :], start=True, stop=True)
                    ins.then_inc(prep_raw, 1)
                    k += 1
            pe.wait_ge(prep_free, 2 * PREP)
            pe.wait_ge(vo_free, 4)
            pe.wait_ge(dve_ready, 1 + 2 * (KVG + KC * KVG + 2))
            pe.wait_ge(dve_step, DVE_STEPS)

            def turn_context(it, j):
                st = stream(j)
                pe.wait_ge(load_c[st], 16 * (round_of(it, j) + 1))
                for kc in range(KC):
                    ins = pe.transpose(misc[:, kc * S:(kc + 1) * S], ctx_nat[st][:, kc * P:(kc + 1) * P], ident[0:S, 0:S])
                ins.then_inc(sems["ct_raw"], 1)

            def turn_x(it, j):
                st = stream(j)
                pe.wait_ge(load_x[st], 16 * (round_of(it, j) + 1))
                pe.transpose(misc[:, 0:T], x_nat[st][:, :], ident[:, :]).then_inc(sems["x_in"], 1)

            def context_chunk(it, j, k):
                st, n = stream(j), layer(j) // 2
                b = bank_of(j, k)
                if k == 0 and layer(j) == 0:
                    pe.wait_ge(sems["ct_lo"], at("ct_lo", it, j, 1))
                fam = chunk_sem(j, k)[0]
                if last := bank_before(it, j, k):
                    prev, i = chunk_sem(*last)
                    pe.wait_ge(sems[prev + "_lo"], at(prev + "_lo", it, last[0], i + 1))
                ct = ctx_t[st]
                if is_gqa(j) and k == 0:
                    for g in range(KVG):
                        ins = split_product(ring_c[:, b, g * S:(g + 1) * S],
                                            [(hl(lambda i: wk_r[n][:, i, kc, g].rearrange("p a d -> p (a d)")), hl(lambda i: ct[:, i, kc, :]))
                                             for kc in range(KC)])
                elif is_gqa(j):
                    ins = split_product(ring_c[0:S, b, 0:KVG * GD],
                                        [(hl(lambda i: ct[:, i, kc, :]), hl(lambda i: wv_g[n][:, i, kc, :])) for kc in range(KC)])
                elif k < len(G_CHUNKS):
                    h0, h1 = G_CHUNKS[k]
                    for h in range(h0, h1):
                        ins = split_product(ring_c[:, b, (h - h0) * S:(h - h0 + 1) * S],
                                            [(hl(lambda i: m_w[n][:, i, m_place(h), kc, :]), hl(lambda i: ct[:, i, kc, :])) for kc in range(KC)])
                else:
                    n0, n1 = V_CHUNKS[k - len(G_CHUNKS)]
                    ins = split_product(ring_c[0:S, b, :],
                                        [(hl(lambda i: ct[:, i, kc, :]), hl(lambda i: wv_m[n][:, i, kc, n0:n1])) for kc in range(KC)])
                ins.then_inc(sems[fam + "_raw"], 1)

            def turn_probs(it, j, x, half):
                if x == HI and half == 0:
                    pe.wait_ge(sems["p_hi"], at("p_hi", it, j, 1))
                if x == LO:
                    if half == 0:
                        pe.wait_ge(sems["p_lo"], at("p_lo", it, j, 1))
                    pe.wait_ge(sems["turn_hi"], at("turn_hi", it, j, half + 1))
                elif exists(it, j - 1) and half < PER_ITEM["ot_lo"][layer(j - 1)]:
                    pe.wait_ge(sems["ot_lo"], at("ot_lo", it, j - 1, half + 1))
                for m in range(TURN):
                    h = half * TURN + m
                    ins = pe.transpose(ring_th[half][:, m * T:(m + 1) * T], p_s[j % 2][:, x, h * S:h * S + P], ident_h[:, :])
                ins.then_inc(sems["turn_raw"], 1)

            def values(it, j, k):
                if k == 0:
                    pe.wait_ge(sems["turn_hi"], at("turn_hi", it, j, 2))
                    if not is_gqa(j):
                        pe.wait_ge(sems["cv_lo"], at("cv_lo", it, j, 1))
                    else:
                        pe.wait_ge(sems["ctx_lo"], at("ctx_lo", it, j, 2))
                pe.wait_ge(sems[f"turn_lo{k}"], at(f"turn_lo{k}", it, j, 1))
                for h in range(k * TURN, (k + 1) * TURN):
                    if is_gqa(j):
                        out, v = so_flat[:, h * (GD + 1):(h + 1) * (GD + 1)], hl(lambda i: v_gqa[j // 2 % 2][:, i, h // R, :])
                    else:
                        o = (h % HEADS_O) * (MD + 1)
                        out, v = so[:, h // HEADS_O, o:o + MD + 1], hl(lambda i: v_mha[j // 2 % 2][:, i, h, :])
                    ins = split_product(out, [(hl(lambda i: p_t[:, i, h, :]), v)])
                    if h == H - 1 or (h == 2 * HEADS_O - 1 and not is_gqa(j)):
                        ins.then_inc(sems["o_raw"], 1)

            def turn_o(it, j, k):
                pe.wait_ge(sems["o_norm"], at("o_norm", it, j, k + 1))
                for m in range(1 if is_gqa(j) else OTURN):
                    ins = pe.transpose(ring_t[:, k, m * T:(m + 1) * T], o_n[:, k * OTURN + m, :], ident[:, :])
                ins.then_inc(sems["ot_raw"], 1)

            def output(it, j):
                n = layer(j) // 2
                pe.wait_ge(sems["ot_lo"], at("ot_lo", it, j, PER_ITEM["ot_lo"][layer(j)]))
                if is_gqa(j):
                    terms = [(hl(lambda i: wo_g[n][:, i, :]), hl(lambda i: o_t[:, i, 0, :]))]
                else:
                    terms = [(hl(lambda i: wo_m[n][:, i, c, :]), hl(lambda i: o_t[:, i, c, :])) for c in range(NOC)]
                if layer(j) == LAYERS - 1:
                    terms = [(b, a) for a, b in terms]
                split_product(misc[:, 0:P], terms).then_inc(sems["y_raw"], 1)

            def scores(it, j):
                st, n = stream(j), layer(j) // 2
                if is_gqa(j):
                    pe.wait_ge(sems["sq"], at("sq", it, j, 1))
                    pe.matmul(so_flat[:, SS_COL:SS_COL + 1], x_sq[st][:, :], ones[:, :], start=True, stop=True)
                    pe.wait_ge(sems["kb"], at("kb", it, j, 1))
                    pe.wait_ge(sems["q_lo"], at("q_lo", it, j, 1))
                    kb = k_bd[:, :, :, :].rearrange("p g r s -> p (g r s)")
                    for g in range(KVG):
                        a = g * R * S
                        while a < (g + 1) * R * S:
                            e = min((g + 1) * R * S, (a // BANK + 1) * BANK)
                            ins = pe.matmul(so_flat[:, a:e], q_rep[:, g, :], kb[:, a:e], start=True, stop=True)
                            a = e
                else:
                    pe.wait_ge(sems["xm_lo"], at("xm_lo", it, j, 1))
                    pe.wait_ge(sems["ctx_lo"], at("ctx_lo", it, j, len(G_CHUNKS)))
                    ind = bias_r[n][:, :, :].rearrange("p h s -> p (h s)")
                    for a in range(0, HS, BANK):
                        e = min(HS, a + BANK)
                        pe.matmul(so_flat[:, a:e], bias_l[:, :], ind[:, a:e], start=True, stop=False)
                        for x, y in ((HI, HI), (HI, LO), (LO, HI)):
                            ins = pe.matmul(so_flat[:, a:e], x_s[st][:, x, :], g_s[:, y, a:e], start=False, stop=(x == LO))
                ins.then_inc(sems["s_raw"], 1)

            def queries(it, j):
                st, n = stream(j), layer(j) // 2
                pe.wait_ge(sems["xg_lo"], at("xg_lo", it, j, 1))
                for g in range(KVG):
                    ins = split_product(misc[:, g * T:(g + 1) * T],
                                        [(hl(lambda i: wq_r[n][:, i, g].rearrange("p a d -> p (a d)")), hl(lambda i: x_s[st][:, i, :]))])
                ins.then_inc(sems["q_raw"], 1)

            def misc_free(it, j, kind):
                if before := misc_before(it, j, kind):
                    pe.wait_ge(sems[before[0]], at(before[0], it, before[1], 1))

            def slot(it, j):
                c, p, o, e = j + 1, j - 1, j - 2, j + 2
                if exists(it, j):
                    scores(it, j)
                if exists(it, o) and layer(o) == LAYERS - 1:
                    misc_free(it, j, "xr")
                    pe.wait_ge(sems["xb"], at("xb", it, o, 1))
                    pe.transpose(misc[:, 0:D], x_b[stream(o)][:, :], ident[:, :]).then_inc(sems["xr_raw"], 1)
                if exists(it, p):
                    turn_probs(it, p, HI, 0)
                    turn_probs(it, p, HI, 1)
                for item, k in chunks_before(j):
                    if exists(it, item):
                        context_chunk(it, item, k)
                if exists(it, p):
                    turn_probs(it, p, LO, 0)
                    turn_probs(it, p, LO, 1)
                if exists(it, o):
                    misc_free(it, j, "y")
                    output(it, o)
                if exists(it, p):
                    if exists(it, j):
                        pe.wait_ge(sems["s_sub"], at("s_sub", it, j, 1))
                    values(it, p, 0)
                    values(it, p, 1)
                after = [a for a in chunks_after(j) if exists(it, a[0])]
                if is_gqa(c):
                    if exists(it, c):
                        misc_free(it, j, "q")
                        queries(it, c)
                    for item, k in after[:1]:
                        context_chunk(it, item, k)
                    if exists(it, p):
                        turn_o(it, p, 0)
                    for item, k in after[1:]:
                        context_chunk(it, item, k)
                    return
                first = layer(e) == 0 and exists(it, e)
                for item, k in after[:1]:
                    context_chunk(it, item, k)
                if first:
                    misc_free(it, j, "x")
                    turn_x(it, e)
                for item, k in after[1:2]:
                    context_chunk(it, item, k)
                if exists(it, p):
                    for k in range(NOT):
                        turn_o(it, p, k)
                for item, k in after[2:]:
                    context_chunk(it, item, k)
                if first:
                    misc_free(it, j, "ct")
                    turn_context(it, e)

            for j in range(-2, SLOTS):
                slot(0, j)
            with pe.Fori(1, NIT - 1) as it:
                for j in range(SLOTS):
                    slot(it, j)
            for j in range(SLOTS):
                slot(NIT - 1, j)
            for j in range(TAIL):
                slot(NIT, j)


CONSTS = 15
ARENA = 9216
SMALL_LOADS = 20
DVE_STEPS = 52


_GQA = ("wq", "wk", "wv", "wo", "norm_w")
_MHA = {"Wq": "Wq", "Wk": "Wk", "Wv": "Wv", "Wo": "Wo", "bo": "bo",
        "tok_a": "token_indices_A", "tok_b": "token_indices_B"}


def kernel(**inputs):
    import numpy as _np
    import concourse.bacc as _bacc
    from concourse import mybir as _mybir
    from concourse.bass_utils import run_bass_kernel_spmd as _run

    nc = _bacc.Bacc("TRN2", target_bir_lowering=False, num_devices=1)
    arrays = {}

    def given(name):
        a = _np.ascontiguousarray(inputs[name])
        arrays[f"in_{name}_dram"] = a
        return nc.dram_tensor(f"in_{name}_dram", a.shape, _mybir.dt.from_np(a.dtype), kind="ExternalInput").ap()

    x, ctx = given("x"), given("ctx_2048")
    mask_a, mask_b = given("mask_S_fk1"), given("mask_S_fk0")
    gqa = [{k: given(f"L{n}_xattn_{k}") for k in _GQA} for n in (0, 2)]
    mha = [{k: given(f"L{n}_xattn_{v}") for k, v in _MHA.items()} for n in (1, 3)]
    out = nc.dram_tensor("out_0_dram", x.shape, _mybir.dt.float32, kind="ExternalOutput").ap()
    build(nc, x, ctx, mask_a, mask_b, gqa, mha, out)
    r = _run(nc, [arrays], core_ids=[0])
    return r.results[0]["out_0_dram"]
```

```python
from contextlib import ExitStack

import numpy as np

import concourse.bass as bass
from concourse import mybir

ALU = mybir.AluOpType
ACT = mybir.ActivationFunctionType
AX_X = mybir.AxisListType.X
F32 = mybir.dt.float32
F16 = mybir.dt.float16
BF16 = mybir.dt.bfloat16
I32 = mybir.dt.int32

P = 128
H = 16
EPS = 1e-5
SUPPRESS = 20.0
STREAMS = 4
LAYERS = 4
SLOTS = STREAMS * LAYERS
PLACES = [0, 3, 8, 11]
ITEMS = [next((st, la, int(2 * st + PLACES[la] >= SLOTS)) for st in range(STREAMS) for la in range(LAYERS)
              if (2 * st + PLACES[la]) % SLOTS == j) for j in range(SLOTS)]
HI, LO = 0, 1


def build(nc, x_d, ctx_d, mask_a_d, mask_b_d, gqa_w, mha_w, out_d):
    B, T, D = x_d.shape
    S, C = ctx_d.shape[1:]
    KC = C // P
    GD = D // H
    KVG = gqa_w[0]["wk"].shape[1] // GD
    R = H // KVG
    INNER = mha_w[0]["Wq"].shape[1]
    MD = INNER // H
    NOC = INNER // P
    HPC = P // MD
    HS = H * S
    BANK = 512
    NIT = B // STREAMS
    TAIL = max(j for j in range(SLOTS) if ITEMS[j][2]) + 4
    assert T == P and D == P and GD * R * 4 == P and HS <= 3 * BANK

    W_GQA = 16.0
    W_M = 16.0
    W_V = 64.0
    W_P = 4096.0
    MHA_SCALE = float(MD) ** -0.5 / W_M
    Y_SCALE = 1.0 / (W_V * W_V)
    SS_MUL = GD * W_GQA ** 4 / D
    SS_ADD = GD * W_GQA ** 4 * EPS

    def stream(j):
        return ITEMS[j % SLOTS][0]

    def layer(j):
        return ITEMS[j % SLOTS][1]

    def is_gqa(j):
        return layer(j) % 2 == 0

    def following(j):
        return j + (3 if is_gqa(j) else 5)

    def m_place(h):
        return h % HPC * NOC + h // HPC

    def round_of(it, j):
        return it + j // SLOTS - ITEMS[j % SLOTS][2]

    def exists(it, j):
        return not isinstance(it, int) or 0 <= round_of(it, j) < NIT

    HEADS_G = BANK // S
    G_CHUNKS = [(h, min(H, h + HEADS_G)) for h in range(0, H, HEADS_G)]
    V_CHUNKS = [(n, n + BANK) for n in range(0, INNER, BANK)]
    HEADS_O = 6
    HALF = H // 2

    gqa_only, mha_only = (1, 0, 1, 0), (0, 1, 0, 1)
    dma = (16,) * 4
    first_only, last_only, each, two = (1, 0, 0, 0), (0, 0, 0, 1), (1, 1, 1, 1), (2, 2, 2, 2)
    NG = len(G_CHUNKS)
    n_ctx = (1, NG) * 2
    n_cv = (0, len(V_CHUNKS)) * 2
    n_o = (1, 2, 1, 2)
    mha_dma = (0, 16, 0, 16)
    whole = [h for h in (BANK // S, 2 * BANK // S, H)]
    MAX_STEPS = {True: [(0, H)], False: list(zip([0] + whole[:2], whole))}
    n_s = (1, 3, 1, 3)
    PER_ITEM = {
        "q_raw": gqa_only, "q_hi": gqa_only, "q_lo": gqa_only, "kb": gqa_only,
        "ms": gqa_only, "rstd": gqa_only, "sq": gqa_only, "xb": mha_only,
        "s_raw": n_s, "s_max": n_s, "s_sub": two, "p_exp": two, "p_hi": two, "p_lo": two,
        "ctx_raw": n_ctx, "ctx_hi": n_ctx, "ctx_lo": n_ctx,
        "cv_raw": n_cv, "cv_hi": n_cv, "cv_lo": n_cv,
        "turned_hi0": dma, "turned_hi1": dma, "turned_lo0": dma, "turned_lo1": dma,
        "ot_raw": gqa_only, "ot_hi": gqa_only, "ot_lo": gqa_only,
        "o_hi": mha_only, "o_lo": mha_only, "turned_o_hi": mha_dma, "turned_o_lo": mha_dma,
        "o_raw": n_o, "o_rcp": two, "o_norm": n_o,
        "yg_raw": gqa_only, "ym_raw": mha_only, "xg_f32": gqa_only, "xg_hi": gqa_only, "xg_lo": gqa_only,
        "xm_f32": mha_only, "xm_hi": mha_only, "xm_lo": mha_only,
        "x_in": first_only, "ct_raw": first_only, "ct_hi": first_only, "ct_lo": first_only,
        "xr_raw": last_only, "xr": last_only, "out": last_only,
    }

    def at(name, it, j, k):
        per = [PER_ITEM[name][ITEMS[n][1]] for n in range(SLOTS)]
        late = [PER_ITEM[name][ITEMS[n][1]] * ITEMS[n][2] for n in range(SLOTS)]
        it, j = it + j // SLOTS, j % SLOTS
        if isinstance(it, int) and it <= 0:
            return sum(per[:j]) - sum(late[:j]) + k if it == 0 else 0
        if isinstance(it, int) and it == NIT:
            return it * sum(per) - sum(late) + sum(late[:j]) + k
        return it * sum(per) - sum(late) + sum(per[:j]) + k

    def chunks(j):
        if is_gqa(j):
            return [(j + 1, "ctx", k) for k in range(NG)]
        return [(j + 1, "ctx", 0)] + [(j, "cv", k) for k in range(len(V_CHUNKS))]

    assert NG == 3 and len(V_CHUNKS) == 2

    def bank_of(j, fam, k):
        return k % 2 if fam == "cv" or not is_gqa(j) else 1

    def bank_before(it, j, fam, k):
        slot = j if fam == "cv" else j - 1
        order = [c for q in range(slot - 4, slot + 1) for c in chunks(q)]
        place = order.index((j, fam, k)) - 2
        while place >= 0:
            item = order[place][0]
            if exists(it, item) and not (isinstance(it, int) and it * SLOTS + item < 0):
                return order[place]
            place -= 2
        return None

    def x_sem(j, part):
        return ("xg_" if is_gqa(j) else "xm_") + part

    with ExitStack() as ctx:
        def sb(name, shape, dt):
            return ctx.enter_context(nc.sbuf_tensor(name, shape, dt))

        def ps(name, shape):
            return ctx.enter_context(nc.psum_tensor(name, shape, F32))

        def sem(name):
            return ctx.enter_context(nc.semaphore(name))

        wq_r = [sb(f"wq_r{n}", [P, 2, KVG, 4, R * GD], F16) for n in range(2)]
        wk_r = [sb(f"wk_r{n}", [P, 2, KC, KVG, 4 * R, GD], F16) for n in range(2)]
        wv_g = [sb(f"wv_g{n}", [P, 2, KC, KVG * GD], F16) for n in range(2)]
        wo_g = [sb(f"wo_g{n}", [P, 2, D], F16) for n in range(2)]
        m_w = [sb(f"m_w{n}", [P, 2, H, KC, D], F16) for n in range(2)]
        wv_m = [sb(f"wv_m{n}", [P, 2, KC, INNER], F16) for n in range(2)]
        wo_m = [sb(f"wo_m{n}", [P, 2, NOC, D], F16) for n in range(2)]
        norm_w = sb("norm_w", [P, 2], F32)
        bo = sb("bo", [P, 2], F32)
        arena = sb("arena", [P, ARENA], F32)
        taken = [0]

        def in_arena(width, dt):
            words = width if dt == F32 else (width + 1) // 2
            view = arena[:, taken[0]:taken[0] + words]
            taken[0] += words
            assert taken[0] <= ARENA
            return view if dt == F32 else view.bitcast(dt)[:, 0:width]

        st_wq = in_arena(INNER, F32)
        st_wk = in_arena(KC * INNER, F32).rearrange("p (k n) -> p k n", k=KC)
        st_wv = in_arena(KC * INNER, F32).rearrange("p (k n) -> p k n", k=KC)
        st_wo = in_arena(NOC * D, F32).rearrange("p (k n) -> p k n", k=NOC)
        wq_t = in_arena(NOC * D, F32).rearrange("p (a b) -> p a b", a=NOC)
        wk_t = in_arena(NOC * C, F32).rearrange("p (a b) -> p a b", a=NOC)
        taken[0] = 0
        g_s = in_arena(2 * HS, F16).rearrange("p (a n) -> p a n", a=2)
        k_bd = in_arena(HS, F16).rearrange("p (g r s) -> p g r s", g=KVG, s=S)
        probs = in_arena(HS, F32).rearrange("p (h s) -> p h s", s=S)
        shifted = in_arena(HS, F32).rearrange("p (h s) -> p h s", s=S)
        p_t = [in_arena(2 * H * T, F16).rearrange("p (a h t) -> p a h t", a=2, t=T) for n in range(2)]
        o_n = in_arena(NOC * P, F32)
        o_s = in_arena(2 * NOC * P, F16).rearrange("p (a n) -> p a n", a=2)
        o_t = in_arena(2 * NOC * T, F16).rearrange("p (a c t) -> p a c t", a=2, t=T)
        st_gq = sb("st_gq", [P, 2, D], F32)
        st_gk = sb("st_gk", [P, 2, KC, KVG * GD], F32)
        st_gv = sb("st_gv", [P, 2, KC, KVG * GD], F32)
        st_go = sb("st_go", [P, 2, D], F32)
        ident = sb("ident", [P, P], F32)
        ident_h = sb("ident_h", [P, P], F16)
        log_w = sb("log_w", [P, 1], F32)
        ones = sb("ones", [P, 1], F32)
        minus_half = sb("minus_half", [P, 1], F32)
        part_i = sb("part_i", [P, 1], I32)
        part_f = sb("part_f", [P, 2], F32)
        head_i = sb("head_i", [P, 1], I32)
        head_mask = sb("head_mask", [P, R], F32)
        key_i = sb("key_i", [P, S], I32)
        key_f = sb("key_f", [P, S], F32)
        tok_i = sb("tok_i", [6, 4, 2], I32)
        tok_f = sb("tok_f", [6, 4, 2], F32)
        tok_w = sb("tok_w", [6, 4, 2], F32)
        hit = sb("hit", [6, 4, 2, S], F32)
        hit_any = sb("hit_any", [6, 4, S], F32)
        row_sel = sb("row_sel", [6, 8], F32)
        mask_r = sb("mask_r", [6, 8, P], F32)
        mask_p = sb("mask_p", [6, 3, P], BF16)
        bias_l = sb("bias_l", [P, P], BF16)
        bias_r = [sb(f"bias_r{n}", [P, H, S], BF16) for n in range(2)]
        x_nat = [sb(f"x_nat{n}", [P, D], F32) for n in range(STREAMS)]
        ctx_nat = [sb(f"ctx_nat{n}", [S, C], F32) for n in range(STREAMS)]
        ctx_t = [sb(f"ctx_t{n}", [P, 2, KC, S], F16) for n in range(STREAMS)]
        x_f = [sb(f"x_f{n}", [P, T], F32) for n in range(STREAMS)]
        x_b = [sb(f"x_b{n}", [P, T], F32) for n in range(STREAMS)]
        x_s = [sb(f"x_s{n}", [P, 2, T], F16) for n in range(STREAMS)]
        x_sq = [sb(f"x_sq{n}", [P, T], F32) for n in range(STREAMS)]
        y_out = [sb(f"y_out{n}", [P, D], F32) for n in range(STREAMS)]
        v_gqa = [sb(f"v_gqa{n}", [P, KVG, 2, GD + 1], F16) for n in range(2)]
        v_mha = [sb(f"v_mha{n}", [P, 2, H, MD + 1], F16) for n in range(2)]
        p_s = [sb(f"p_s{n}", [P, 2, H, P], F16) for n in range(2)]
        ms = sb("ms", [P, 2], F32)
        rstd = sb("rstd", [P, 2], F32)
        o_ng = sb("o_ng", [P, P], F32)
        o_tg = sb("o_tg", [P, 2, T], F16)
        k_rep = sb("k_rep", [P, KVG, S], F16)
        q_rep = sb("q_rep", [P, KVG, T], F16)
        row_max = sb("row_max", [P, H], F32)
        den_r = sb("den_r", [P, 3 * HEADS_O], F32)
        x_res = sb("x_res", [P, D], F32)

        so = ps("so", [P, 3, BANK])
        ring_c = ps("ring_c", [P, 2, BANK])
        ring_t = ps("ring_t", [P, 2, BANK])
        misc = ps("misc", [P, BANK])
        so_flat = so[:, :, :].rearrange("p b n -> p (b n)")
        s_view = so_flat[:, 0:HS].rearrange("p (h s) -> p h s", s=S)
        V_COL = KVG * S
        X_IN, Y_GQA = slice(0, T), slice(P, 2 * P)
        X_RES = slice(2 * P, 2 * P + D)
        SS_COL = HS + 64

        sems = {name: sem(name) for name in PER_ITEM}
        load_x = [sem(f"load_x{n}") for n in range(STREAMS)]
        load_c = [sem(f"load_c{n}") for n in range(STREAMS)]
        stored = [sem(f"stored{n}") for n in range(STREAMS)]
        load_small = sem("load_small")
        load_qk = sem("load_qk")
        load_vo = sem("load_vo")
        vo_free = sem("vo_free")
        consts_pool = sem("consts_pool")
        pool_step = sem("pool_step")
        dve_step = sem("dve_step")
        ident_ready = sem("ident_ready")
        split_gqa = sem("split_gqa")
        split_vo = sem("split_vo")
        dve_ready = sem("dve_ready")
        prep_raw = sem("prep_raw")
        prep_hi = sem("prep_hi")
        prep_free = sem("prep_free")

        prep_banks = [t[:, n, :] for t, size in ((ring_t, 2), (ring_c, 2), (so, 3)) for n in range(size)] + [misc[:, :]]
        NB = len(prep_banks)
        NTQ = NOC // 4
        NTK = NOC * KC // 4
        NMM = H * KC // 4
        PREP = NTQ + NTK + NMM

        block = ctx.enter_context(nc.Block())

        @block.sync
        def _(sp):
            def load_mha(n):
                if n:
                    sp.wait_ge(prep_raw, NTQ + NTK)
                sp.dma_start(st_wq, mha_w[n]["Wq"]).then_inc(load_qk, 16)
                sp.dma_start(st_wk, mha_w[n]["Wk"].rearrange("(k p) n -> p k n", p=P)).then_inc(load_qk, 16)
                if n:
                    sp.wait_ge(vo_free, 2)
                sp.dma_start(st_wv, mha_w[n]["Wv"].rearrange("(k p) n -> p k n", p=P)).then_inc(load_vo, 16)
                sp.dma_start(st_wo, mha_w[n]["Wo"].rearrange("(k p) n -> p k n", p=P)).then_inc(load_vo, 16)

            load_mha(0)
            n_small = 0
            for row, d in ((0, mask_a_d), (3, mask_b_d)):
                sp.dma_start(mask_r[row:row + 3, 0, :],
                             d.rearrange("(a t) -> a t", a=1).to_broadcast([3, T])).then_inc(load_small, 16)
                n_small += 1
            for n in range(2):
                for row, d in ((0, mha_w[n]["tok_a"]), (3, mha_w[n]["tok_b"])):
                    sp.dma_start(tok_i[row:row + 3, 2 * n, :],
                                 d.rearrange("(a t) -> a t", a=1).to_broadcast([3, 2])).then_inc(load_small, 16)
                sp.dma_start(tok_i[0:6, 2 * n + 1, :],
                             mha_w[n]["tok_b"].rearrange("(a t) -> a t", a=1).to_broadcast([6, 2])).then_inc(load_small, 16)
                sp.dma_start(norm_w[:, n:n + 1], gqa_w[n]["norm_w"].rearrange("(p a) -> p a", a=1)).then_inc(load_small, 16)
                sp.dma_start(bo[:, n:n + 1], mha_w[n]["bo"].rearrange("(p a) -> p a", a=1)).then_inc(load_small, 16)
                sp.dma_start(st_gq[:, n, :], gqa_w[n]["wq"]).then_inc(load_small, 16)
                sp.dma_start(st_gk[:, n, :, :], gqa_w[n]["wk"].rearrange("(k p) n -> p k n", p=P)).then_inc(load_small, 16)
                sp.dma_start(st_gv[:, n, :, :], gqa_w[n]["wv"].rearrange("(k p) n -> p k n", p=P)).then_inc(load_small, 16)
                sp.dma_start(st_go[:, n, :], gqa_w[n]["wo"]).then_inc(load_small, 16)
                n_small += 9
            assert n_small == SMALL_LOADS
            load_mha(1)
            for st in range(STREAMS):
                sp.dma_start(x_nat[st][:, :], x_d[st, :, :]).then_inc(load_x[st], 16)
                sp.dma_start(ctx_nat[st][:, :], ctx_d[st, :, :]).then_inc(load_c[st], 16)

            def turn(it, j, part, half):
                x = (HI, LO)[part == "lo"]
                name = f"turned_{part}{half}"
                sp.wait_ge(sems["p_" + part], at("p_" + part, it, j, half + 1))
                sp.nop(nofuse=True)
                if part == "hi" and half == 0 and exists(it, j - 2):
                    sp.wait_ge(sems["o_raw"], at("o_raw", it, j - 2, n_o[layer(j - 2)]))
                    sp.nop(nofuse=True)
                if exists(it, j - 1):
                    sp.wait_ge(sems[name], at(name, it, j - 1, 16))
                    sp.nop(nofuse=True)
                hs = slice(half * HALF, (half + 1) * HALF)
                sp.dma_start(p_t[j % 2][:, x, hs, :], p_s[j % 2][:, x, hs, :].rearrange("p h s -> p (h s)"), transpose=True).then_inc(sems[name], 16)

            def turn_out(it, j):
                for x, part in ((HI, "hi"), (LO, "lo")):
                    sp.wait_ge(sems["o_" + part], at("o_" + part, it, j, 1))
                    sp.nop(nofuse=True)
                    if exists(it, j - 2):
                        sp.wait_ge(sems["ym_raw"], at("ym_raw", it, j - 2, 1))
                        sp.nop(nofuse=True)
                        sp.wait_ge(sems["turned_o_" + part], at("turned_o_" + part, it, j - 2, 16))
                        sp.nop(nofuse=True)
                    sp.dma_start(o_t[:, x, :, :], o_s[:, x, :], transpose=True).then_inc(sems["turned_o_" + part], 16)

            def slot(it, j):
                e, o, u = j + 2, j - 2, j - 3
                more = layer(e) == 0 and exists(it, e) and exists(it + 1, e)
                st, n = stream(e), round_of(it, e) + 1
                if not is_gqa(j) and exists(it, o):
                    turn_out(it, o)
                if more:
                    sp.wait_ge(sems["x_in"], at("x_in", it, e, 1))
                    sp.dma_start(x_nat[st][:, :], x_d[n * STREAMS + st, :, :]).then_inc(load_x[st], 16)
                    sp.wait_ge(sems["ct_raw"], at("ct_raw", it, e, 1))
                    sp.dma_start(ctx_nat[st][:, :], ctx_d[n * STREAMS + st, :, :]).then_inc(load_c[st], 16)
                if exists(it, j):
                    for part in ("hi", "lo"):
                        for half in range(2):
                            turn(it, j, part, half)
                if layer(u) == LAYERS - 1 and exists(it, u):
                    sp.wait_ge(sems["out"], at("out", it, u, 1))
                    sp.dma_start(out_d[round_of(it, u) * STREAMS + stream(u), :, :], y_out[stream(u)][:, :]).then_inc(stored[stream(u)], 16)

            for j in range(-2, SLOTS):
                slot(0, j)
            with sp.Fori(1, NIT - 2) as it:
                for j in range(SLOTS):
                    slot(it, j)
            for j in range(2 * SLOTS):
                slot(NIT - 2 + j // SLOTS, j % SLOTS)
            for j in range(TAIL):
                slot(NIT, j)
            for st in range(STREAMS):
                sp.wait_ge(stored[st], 16 * (NIT + 1))

        @block.gpsimd
        def _(pool):
            pool.memset(ident[:, :], 0.0).then_inc(pool_step, 1)
            pool.wait_ge(pool_step, 1)
            pool.affine_select(out=ident[:, :], in_=ident[:, :], compare_op=ALU.not_equal, fill=1.0, base=0,
                               pattern=[[-1, P]], channel_multiplier=1).then_inc(ident_ready, 1)
            pool.memset(ones[:, :], 1.0).then_inc(consts_pool, 1)
            pool.memset(minus_half[:, :], -0.5).then_inc(consts_pool, 1)
            pool.iota(part_i[:, :], pattern=[[0, 1]], base=0, channel_multiplier=1).then_inc(consts_pool, 1)
            pool.iota(key_i[:, :], pattern=[[1, S]], base=0, channel_multiplier=0).then_inc(consts_pool, 1)
            pool.memset(bias_l[:, :], 0.0).then_inc(consts_pool, 1)
            for n in range(2):
                pool.memset(bias_r[n][:, :, :], 0.0).then_inc(consts_pool, 1)
                pool.memset(p_s[n][:, :, :, S:P], 0.0).then_inc(consts_pool, 1)
            pool.memset(log_w[:, :], float(np.log(W_P))).then_inc(consts_pool, 1)
            for n in range(2):
                pool.memset(v_gqa[n][:, :, :, :], 0.0).then_inc(pool_step, 1)
                pool.memset(v_mha[n][:, :, :, :], 0.0).then_inc(pool_step, 1)
            for n in range(STREAMS):
                pool.memset(y_out[n][:, :], 0.0).then_inc(stored[n], 16)
            pool.wait_ge(pool_step, 5)
            for n in range(2):
                pool.memset(v_gqa[n][0:S, :, HI, GD:GD + 1], 1.0).then_inc(consts_pool, 1)
                pool.memset(v_mha[n][0:S, HI, :, MD:MD + 1], 1.0).then_inc(consts_pool, 1)
            pool.wait_ge(ident_ready, 1)
            pool.tensor_copy(ident_h[:, :], ident[:, :]).then_inc(consts_pool, 1)
            pool.wait_ge(load_small, 16 * SMALL_LOADS)

            def x_parts(it, j):
                st = stream(j)
                pool.wait_ge(sems[x_sem(j, "f32")], at(x_sem(j, "f32"), it, j, 1))
                if is_gqa(j):
                    pool.tensor_tensor(x_sq[st][:, :], x_f[st][:, :], x_f[st][:, :], ALU.mult).then_inc(sems["sq"], 1)
                else:
                    n = layer(j) // 2
                    pool.tensor_tensor(x_b[st][:, :], x_f[st][:, :], bo[:, n:n + 1].to_broadcast([P, T]), ALU.add).then_inc(sems["xb"], 1)
                pool.tensor_copy(x_s[st][:, HI, :], x_f[st][:, :]).then_inc(sems[x_sem(j, "hi")], 1)
                pool.wait_ge(sems[x_sem(j, "hi")], at(x_sem(j, "hi"), it, j, 1))
                pool.tensor_tensor(x_s[st][:, LO, :], x_f[st][:, :], x_s[st][:, HI, :], ALU.subtract).then_inc(sems[x_sem(j, "lo")], 1)

            def slot(it, j):
                par, p, o, e, u = j % 2, j - 1, j - 2, j + 2, j - 3
                if is_gqa(j) and exists(it, j):
                    r = j // 2 % 2
                    pool.wait_ge(sems["ms"], at("ms", it, j, 1))
                    pool.tensor_tensor(rstd[:, r:r + 1], ms[:, r:r + 1], minus_half[:, :], ALU.pow).then_inc(sems["rstd"], 1)
                if is_gqa(o) and exists(it, o):
                    x_parts(it, following(o))
                if exists(it, j):
                    for k in range(2):
                        hs = slice(k * HALF, (k + 1) * HALF)
                        pool.wait_ge(sems["p_hi"], at("p_hi", it, j, k + 1))
                        pool.tensor_tensor(p_s[par][:, LO, hs, 0:S], probs[:, hs, :], p_s[par][:, HI, hs, 0:S], ALU.subtract).then_inc(sems["p_lo"], 1)
                if is_gqa(j):
                    if exists(it, e) and (layer(e) == 0 or exists(it, u)):
                        x_parts(it, e)
                    if exists(it, p):
                        pool.wait_ge(sems["o_hi"], at("o_hi", it, p, 1))
                        pool.tensor_tensor(o_s[:, LO, :], o_n, o_s[:, HI, :], ALU.subtract).then_inc(sems["o_lo"], 1)

            for j in range(-2, SLOTS):
                slot(0, j)
            with pool.Fori(1, NIT - 1) as it:
                for j in range(SLOTS):
                    slot(it, j)
            for j in range(SLOTS):
                slot(NIT - 1, j)
            for j in range(TAIL):
                slot(NIT, j)

        @block.scalar
        def _(act):
            def high(out, in_, scale):
                return act.activation(out, in_, ACT.Copy, scale=scale)

            def split_out(n):
                act.wait_ge(load_vo, 32 * (n + 1))
                high(wv_m[n][:, HI], st_wv, W_V).then_inc(split_vo, 1)
                high(wo_m[n][:, HI], st_wo, W_V).then_inc(split_vo, 1)

            def fold_high(n):
                for c in range(NMM):
                    k = n * PREP + NTQ + NTK + c
                    act.wait_ge(prep_raw, k + 1)
                    high(m_w[n][:, HI].rearrange("p h k c -> p (h k c)")[:, c * BANK:(c + 1) * BANK], prep_banks[k % NB], W_M).then_inc(prep_hi, 1)

            split_out(0)
            fold_high(0)
            act.wait_ge(load_small, 16 * SMALL_LOADS)
            act.wait_ge(dve_ready, 1)
            for n in range(2):
                high(wq_r[n][:, HI], st_gq[:, n, :].rearrange("p (g a e) -> p g a e", g=KVG, a=1).to_broadcast([P, KVG, 4, R * GD]), W_GQA).then_inc(split_gqa, 1)
                for kc in range(KC):
                    high(wk_r[n][:, HI, kc], st_gk[:, n, kc, :].rearrange("p (g a e) -> p g a e", g=KVG, a=1).to_broadcast([P, KVG, 4 * R, GD]), W_GQA).then_inc(split_gqa, 1)
                high(wv_g[n][:, HI], st_gv[:, n, :, :], W_V).then_inc(split_gqa, 1)
                high(wo_g[n][:, HI], st_go[:, n, :], W_V).then_inc(split_gqa, 1)
            split_out(1)
            fold_high(1)

            def turn_context(it, j):
                act.wait_ge(sems["ct_raw"], at("ct_raw", it, j, 1))
                high(ctx_t[stream(j)][:, HI], ring_t[:, 1, 0:KC * S].rearrange("p (k s) -> p k s", s=S), 1.0).then_inc(sems["ct_hi"], 1)

            def context_chunk(it, j, fam, k):
                b = bank_of(j, fam, k)
                act.wait_ge(sems[fam + "_raw"], at(fam + "_raw", it, j, k + 1))
                if is_gqa(j):
                    if not (isinstance(it, int) and at("kb", it, j, 0) == 0):
                        act.wait_ge(sems["kb"], at("kb", it, j, 0))
                    high(k_rep[:, :, :], ring_c[:, b, 0:KVG * S].rearrange("p (g s) -> p g s", s=S), 1.0)
                    ins = high(v_gqa[j // 2 % 2][0:S, :, HI, 0:GD], ring_c[0:S, b, V_COL:V_COL + KVG * GD].rearrange("p (g d) -> p g d", d=GD), 1.0)
                elif fam == "ctx":
                    h0, h1 = G_CHUNKS[k]
                    ins = high(g_s[:, HI, h0 * S:h1 * S], ring_c[:, b, 0:(h1 - h0) * S], 1.0)
                else:
                    n0, n1 = V_CHUNKS[k]
                    ins = high(v_mha[j // 2 % 2][0:S, HI, n0 // MD:n1 // MD, 0:MD], ring_c[0:S, b, :].rearrange("p (h d) -> p h d", d=MD), 1.0)
                ins.then_inc(sems[fam + "_hi"], 1)

            def exponential(it, j, k):
                r, hs = j // 2 % 2, slice(k * HALF, (k + 1) * HALF)
                act.wait_ge(sems["s_sub"], at("s_sub", it, j, k + 1))
                act.activation(probs[:, hs, :], shifted[:, hs, :], ACT.Exp, bias=log_w[:, :],
                               scale=rstd[:, r:r + 1] if is_gqa(j) else MHA_SCALE).then_inc(sems["p_exp"], 1)

            def high_part(it, j, k):
                hs = slice(k * HALF, (k + 1) * HALF)
                act.wait_ge(sems["p_exp"], at("p_exp", it, j, k + 1))
                high(p_s[j % 2][:, HI, hs, 0:S], probs[:, hs, :], 1.0).then_inc(sems["p_hi"], 1)

            def exponentials(it, j):
                if is_gqa(j):
                    act.wait_ge(sems["rstd"], at("rstd", it, j, 1))
                if not (isinstance(it, int) and at("p_lo", it, j, 0) == 0):
                    act.wait_ge(sems["p_lo"], at("p_lo", it, j, 0))
                if exists(it, j - 2):
                    for name in ("hi0", "hi1", "lo0", "lo1"):
                        act.wait_ge(sems["turned_" + name], at("turned_" + name, it, j - 2, 16))
                exponential(it, j, 0)
                high_part(it, j, 0)
                exponential(it, j, 1)
                high_part(it, j, 1)

            def slot(it, j):
                c, p, e, u = j + 1, j - 1, j + 2, j - 3
                mine = [a for a in chunks(j) if exists(it, a[0])]
                if is_gqa(j):
                    if exists(it, u) and layer(u) == LAYERS - 1:
                        act.wait_ge(sems["xr_raw"], at("xr_raw", it, u, 1))
                        if exists(it, u - 2) and layer(u - 2) == LAYERS - 1:
                            act.wait_ge(sems["out"], at("out", it, u - 2, 1))
                        if layer(e) == 0 and exists(it, e):
                            act.wait_ge(sems["ct_raw"], at("ct_raw", it, e, 1))
                        high(x_res[:, :], ring_t[:, 1, X_RES], 1.0).then_inc(sems["xr"], 1)
                    if layer(e) == 0 and exists(it, e):
                        turn_context(it, e)
                    for a in mine[:2]:
                        context_chunk(it, *a)
                    if exists(it, j):
                        exponentials(it, j)
                    for a in mine[2:]:
                        context_chunk(it, *a)
                    if exists(it, p):
                        act.wait_ge(sems["o_norm"], at("o_norm", it, p, 2))
                        if exists(it, p - 2):
                            for part in ("hi", "lo"):
                                act.wait_ge(sems["turned_o_" + part], at("turned_o_" + part, it, p - 2, 16))
                        high(o_s[:, HI, :], o_n, 1.0).then_inc(sems["o_hi"], 1)
                    return
                if exists(it, c):
                    context_chunk(it, c, "ctx", 0)
                if exists(it, j):
                    exponentials(it, j)
                if exists(it, c):
                    act.wait_ge(sems["q_raw"], at("q_raw", it, c, 1))
                    high(q_rep[:, :, :], ring_t[:, 1, :].rearrange("p (g t) -> p g t", t=T), 1.0).then_inc(sems["q_hi"], 1)
                if exists(it, j):
                    context_chunk(it, j, "cv", 0)
                if exists(it, p):
                    act.wait_ge(sems["ot_raw"], at("ot_raw", it, p, 1))
                    high(o_tg[:, HI, :], ring_t[:, 0, 0:T], 1.0).then_inc(sems["ot_hi"], 1)
                if exists(it, j):
                    context_chunk(it, j, "cv", 1)

            for j in range(-2, SLOTS):
                slot(0, j)
            with act.Fori(1, NIT - 1) as it:
                for j in range(SLOTS):
                    slot(it, j)
            for j in range(SLOTS):
                slot(NIT - 1, j)
            for j in range(TAIL):
                slot(NIT, j)

        @block.vector
        def _(dve):
            def low(out, in_, scale, hi):
                return dve.scalar_tensor_tensor(out=out, in0=in_, scalar=scale, in1=hi, op0=ALU.mult, op1=ALU.subtract)

            steps = [0]

            def step(ins):
                steps[0] += 1
                ins.then_inc(dve_step, 1)
                dve.wait_ge(dve_step, steps[0])

            def turned_weights(n):
                for c in range(NTQ + NTK):
                    k = n * PREP + c
                    dve.wait_ge(prep_raw, k + 1)
                    dst = (wq_t if c < NTQ else wk_t).rearrange("p a b -> p (a b)")
                    o = (c if c < NTQ else c - NTQ) * BANK
                    dve.tensor_copy(dst[:, o:o + BANK], prep_banks[k % NB]).then_inc(prep_free, 1)

            def fold_low(n):
                for c in range(NMM):
                    k = n * PREP + NTQ + NTK + c
                    dve.wait_ge(prep_hi, n * NMM + c + 1)
                    part = slice(c * BANK, (c + 1) * BANK)
                    low(m_w[n][:, LO].rearrange("p h k c -> p (h k c)")[:, part], prep_banks[k % NB], W_M,
                        m_w[n][:, HI].rearrange("p h k c -> p (h k c)")[:, part]).then_inc(prep_free, 1)

            def split_out(n):
                dve.wait_ge(split_vo, 2 * (n + 1))
                low(wv_m[n][:, LO], st_wv, W_V, wv_m[n][:, HI]).then_inc(vo_free, 1)
                low(wo_m[n][:, LO], st_wo, W_V, wo_m[n][:, HI]).then_inc(vo_free, 1)

            def selectors():
                step(dve.tensor_copy(part_f[:, 0:1], part_i[:, :]))
                step(dve.tensor_scalar(head_i[:, :], part_i[:, :], int(np.log2(GD)), R - 1, ALU.logical_shift_right, ALU.bitwise_and))
                step(dve.tensor_copy(part_f[:, 1:2], head_i[:, :]))
                for r in range(R):
                    step(dve.tensor_scalar(head_mask[:, r:r + 1], part_f[:, 1:2], float(r), None, ALU.is_equal))
                for k in range(3):
                    step(dve.tensor_scalar(row_sel[:, k:k + 1], part_f[0:6, 0:1], float(k), None, ALU.is_equal))
                    step(dve.tensor_scalar(row_sel[:, 4:5], part_f[0:6, 0:1], float(k + 3), None, ALU.is_equal))
                    step(dve.tensor_tensor(row_sel[:, k:k + 1], row_sel[:, k:k + 1], row_sel[:, 4:5], ALU.add))
                step(dve.tensor_scalar(row_sel[:, 3:4], part_f[0:6, 0:1], 3.0, None, ALU.is_lt))
                tok_flat = tok_f[:, :, :].rearrange("p a b -> p (a b)")
                wrap_flat = tok_w[:, :, :].rearrange("p a b -> p (a b)")
                step(dve.tensor_copy(tok_flat, tok_i[:, :, :].rearrange("p a b -> p (a b)")))
                step(dve.tensor_scalar(wrap_flat, tok_flat, 0.0, float(S), ALU.is_lt, ALU.mult))
                step(dve.tensor_tensor(tok_flat, tok_flat, wrap_flat, ALU.add))
                for a in range(4):
                    for b in range(2):
                        step(dve.tensor_scalar(hit[:, a, b, :], key_f[0:6, :], tok_f[:, a, b:b + 1], None, ALU.is_equal))
                    step(dve.tensor_tensor(hit_any[:, a, :], hit[:, a, 0, :], hit[:, a, 1, :], ALU.max))

            def bias_factors():
                for n in range(2):
                    own, over = hit_any[:, 2 * n, :], hit_any[:, 2 * n + 1, :]
                    step(dve.tensor_scalar(over, over, row_sel[:, 3:4], -1.0, ALU.mult, ALU.mult))
                    step(dve.tensor_scalar(over, over, 1.0, None, ALU.add))
                    step(dve.tensor_tensor(own, own, over, ALU.mult))
                    step(dve.tensor_copy(bias_r[n][0:6, :, :], own.unsqueeze(1).to_broadcast([6, H, S])))
                m = [mask_r[:, k, :] for k in range(8)]
                step(dve.tensor_scalar(m[1], m[0], -1.0, 1.0, ALU.mult, ALU.add))
                step(dve.tensor_scalar(m[2], m[1], -SUPPRESS, 1.0 / MHA_SCALE, ALU.mult, ALU.mult))
                step(dve.tensor_copy(mask_p[:, 0, :], m[2]))
                step(dve.tensor_tensor(m[3], m[2], mask_p[:, 0, :], ALU.subtract))
                step(dve.tensor_copy(mask_p[:, 1, :], m[3]))
                step(dve.tensor_tensor(m[4], m[3], mask_p[:, 1, :], ALU.subtract))
                step(dve.tensor_copy(mask_p[:, 2, :], m[4]))
                step(dve.tensor_scalar(m[5], mask_p[:, 0, :], row_sel[:, 0:1], None, ALU.mult))
                step(dve.scalar_tensor_tensor(out=m[6], in0=mask_p[:, 1, :], scalar=row_sel[:, 1:2], in1=m[5], op0=ALU.mult, op1=ALU.add))
                step(dve.scalar_tensor_tensor(out=bias_l[0:6, :], in0=mask_p[:, 2, :], scalar=row_sel[:, 2:3], in1=m[6], op0=ALU.mult, op1=ALU.add))

            def split_gqa_weights():
                NSPLIT = 3 + KC
                for n in range(2):
                    dve.wait_ge(split_gqa, NSPLIT * (n + 1))
                    for g in range(KVG):
                        low(wq_r[n][:, LO, g], st_gq[:, n, g * R * GD:(g + 1) * R * GD].unsqueeze(1).to_broadcast([P, 4, R * GD]), W_GQA, wq_r[n][:, HI, g]).then_inc(dve_ready, 1)
                    for kc in range(KC):
                        for g in range(KVG):
                            low(wk_r[n][:, LO, kc, g], st_gk[:, n, kc, g * GD:(g + 1) * GD].unsqueeze(1).to_broadcast([P, 4 * R, GD]), W_GQA, wk_r[n][:, HI, kc, g]).then_inc(dve_ready, 1)
                    low(wv_g[n][:, LO], st_gv[:, n, :, :], W_V, wv_g[n][:, HI]).then_inc(dve_ready, 1)
                    low(wo_g[n][:, LO], st_go[:, n, :], W_V, wo_g[n][:, HI]).then_inc(dve_ready, 1)

            turned_weights(0)
            dve.wait_ge(consts_pool, CONSTS)
            dve.wait_ge(load_small, 16 * SMALL_LOADS)
            for n in range(2):
                step(dve.tensor_scalar(st_gq[:, n, :], st_gq[:, n, :], norm_w[:, n:n + 1], None, ALU.mult))
            dve.tensor_copy(key_f[:, :], key_i[:, :]).then_inc(dve_ready, 1)
            split_out(0)
            selectors()
            fold_low(0)
            turned_weights(1)
            bias_factors()
            assert steps[0] == DVE_STEPS, steps[0]
            split_gqa_weights()
            split_out(1)
            fold_low(1)

            def turn_context(it, j):
                st = stream(j)
                dve.wait_ge(sems["ct_hi"], at("ct_hi", it, j, 1))
                low(ctx_t[st][:, LO], ring_t[:, 1, 0:KC * S].rearrange("p (k s) -> p k s", s=S), 1.0, ctx_t[st][:, HI]).then_inc(sems["ct_lo"], 1)

            def context_chunk(it, j, fam, k):
                b = bank_of(j, fam, k)
                dve.wait_ge(sems[fam + "_hi"], at(fam + "_hi", it, j, k + 1))
                if is_gqa(j):
                    raw = ring_c[:, b, 0:KVG * S].rearrange("p (g s) -> p g s", s=S)
                    v = v_gqa[j // 2 % 2]
                    low(k_rep[32:64], raw[32:64], 1.0, k_rep[32:64])
                    low(k_rep[96:128], raw[96:128], 1.0, k_rep[96:128])
                    ins = low(v[0:S, :, LO, 0:GD], ring_c[0:S, b, V_COL:V_COL + KVG * GD].rearrange("p (g d) -> p g d", d=GD), 1.0, v[0:S, :, HI, 0:GD])
                elif fam == "ctx":
                    h0, h1 = G_CHUNKS[k]
                    ins = low(g_s[:, LO, h0 * S:h1 * S], ring_c[:, b, 0:(h1 - h0) * S], 1.0, g_s[:, HI, h0 * S:h1 * S])
                else:
                    n0, n1 = V_CHUNKS[k]
                    v, hs = v_mha[j // 2 % 2], slice(n0 // MD, n1 // MD)
                    ins = low(v[0:S, LO, hs, 0:MD], ring_c[0:S, b, :].rearrange("p (h d) -> p h d", d=MD), 1.0, v[0:S, HI, hs, 0:MD])
                ins.then_inc(sems[fam + "_lo"], 1)

            def spread_keys(it, j):
                dve.wait_ge(sems["ctx_lo"], at("ctx_lo", it, j, 1))
                for r in range(R):
                    ins = dve.tensor_scalar(k_bd[:, :, r, :], k_rep[:, :, :], head_mask[:, r:r + 1], None, ALU.mult)
                ins.then_inc(sems["kb"], 1)

            def normalise(it, j, k):
                dve.wait_ge(sems["o_raw"], at("o_raw", it, j, k + 1))
                if is_gqa(j):
                    o = so_flat[:, 0:H * 2 * (GD + 1)].rearrange("p (h a d) -> p h a d", a=2, d=GD + 1)
                    r = den_r[:, 0:H].unsqueeze(2)
                    dst, width = o_ng[:, :].rearrange("p (h d) -> p h d", d=GD), [P, H, GD]
                    den = o[:, :, HI, GD:GD + 1]
                    dve.reciprocal(r, den)
                    dve.tensor_copy(dst, o[:, :, LO, 0:GD]).then_inc(sems["o_rcp"], 1)
                    dve.wait_ge(sems["o_rcp"], at("o_rcp", it, j, 1))
                    dve.tensor_tensor(dst, dst, o[:, :, HI, 0:GD], ALU.add).then_inc(sems["o_rcp"], 1)
                    dve.wait_ge(sems["o_rcp"], at("o_rcp", it, j, 2))
                    dve.tensor_tensor(dst, dst, r.to_broadcast(width), ALU.mult).then_inc(sems["o_norm"], 1)
                    return
                else:
                    b0, nb, nh = ((0, 2, HEADS_O), (2, 1, H - 2 * HEADS_O))[k]
                    o = so[:, b0:b0 + nb, 0:nh * (MD + 1)].rearrange("p b (h d) -> p b h d", d=MD + 1)
                    h0 = b0 * HEADS_O
                    r = den_r[:, h0:h0 + nb * nh].rearrange("p (b h a) -> p b h a", h=nh, a=1)
                    dst = o_n[:, h0 * MD:(h0 + nb * nh) * MD].rearrange("p (b h d) -> p b h d", h=nh, d=MD)
                    num, den, width = o[:, :, :, 0:MD], o[:, :, :, MD:MD + 1], [P, nb, nh, MD]
                    if k == 0 and exists(it, j - 2):
                        dve.wait_ge(sems["o_lo"], at("o_lo", it, j - 2, 1))
                dve.reciprocal(r, den).then_inc(sems["o_rcp"], 1)
                dve.wait_ge(sems["o_rcp"], at("o_rcp", it, j, k + 1))
                dve.tensor_tensor(dst, num, r.to_broadcast(width), ALU.mult).then_inc(sems["o_norm"], 1)

            def first_x(it, j):
                dve.wait_ge(sems["x_in"], at("x_in", it, j, 1))
                dve.tensor_copy(x_f[stream(j)][:, :], ring_t[:, 0, X_IN]).then_inc(sems["xg_f32"], 1)

            def finish(it, p):
                st = stream(p)
                if is_gqa(p):
                    dve.wait_ge(sems["yg_raw"], at("yg_raw", it, p, 1))
                else:
                    dve.wait_ge(sems["ym_raw"], at("ym_raw", it, p, 1))
                if layer(p) == LAYERS - 1:
                    dve.wait_ge(sems["xr"], at("xr", it, p, 1))
                    dve.wait_ge(stored[st], 16 * (round_of(it, p) + 1))
                    dve.scalar_tensor_tensor(out=y_out[st][:, :], in0=misc[:, 0:D], scalar=Y_SCALE, in1=x_res[:, :],
                                             op0=ALU.mult, op1=ALU.add).then_inc(sems["out"], 1)
                    return
                y, base = ring_t[:, 0, Y_GQA], x_f[st]
                if not is_gqa(p):
                    dve.wait_ge(sems["xb"], at("xb", it, p, 1))
                    y, base = misc[:, 0:T], x_b[st]
                dve.scalar_tensor_tensor(out=x_f[st][:, :], in0=y, scalar=Y_SCALE, in1=base[:, :],
                                         op0=ALU.mult, op1=ALU.add).then_inc(sems[x_sem(following(p), "f32")], 1)

            def softmax_shift(it, j):
                r = j // 2 % 2
                halves = [slice(k * HALF, (k + 1) * HALF) for k in range(2)]
                steps = MAX_STEPS[is_gqa(j)]
                for k, (h0, h1) in enumerate(steps):
                    dve.wait_ge(sems["s_raw"], at("s_raw", it, j, k + 1))
                    if is_gqa(j):
                        dve.tensor_scalar(ms[:, r:r + 1], so_flat[:, SS_COL:SS_COL + 1], SS_MUL, SS_ADD, ALU.mult, ALU.add).then_inc(sems["ms"], 1)
                    dve.tensor_reduce(row_max[:, h0:h1], s_view[:, h0:h1, :], AX_X, ALU.max).then_inc(sems["s_max"], 1)
                for k, hs in enumerate(halves):
                    last = max(n for n, (h0, h1) in enumerate(steps) if h0 < hs.stop)
                    dve.wait_ge(sems["s_max"], at("s_max", it, j, last + 1))
                    if k == 0 and not (isinstance(it, int) and at("p_exp", it, j, 0) == 0):
                        dve.wait_ge(sems["p_exp"], at("p_exp", it, j, 0))
                    dve.tensor_tensor(shifted[:, hs, :], s_view[:, hs, :], row_max[:, hs].unsqueeze(2).to_broadcast([P, HALF, S]),
                                      ALU.subtract).then_inc(sems["s_sub"], 1)

            def slot(it, j):
                c, p, o, e, u = j + 1, j - 1, j - 2, j + 2, j - 3
                mine = [a for a in chunks(j) if exists(it, a[0])]
                if exists(it, j):
                    softmax_shift(it, j)
                if is_gqa(j):
                    if exists(it, o):
                        finish(it, o)
                    if layer(e) == 0 and exists(it, e):
                        first_x(it, e)
                        turn_context(it, e)
                    for a in mine[:2]:
                        context_chunk(it, *a)
                    if exists(it, p):
                        normalise(it, p, 0)
                        normalise(it, p, 1)
                    for a in mine[2:]:
                        context_chunk(it, *a)
                    if exists(it, u):
                        finish(it, u)
                    return
                if exists(it, c):
                    context_chunk(it, c, "ctx", 0)
                    spread_keys(it, c)
                if exists(it, p):
                    normalise(it, p, 0)
                if exists(it, c):
                    dve.wait_ge(sems["q_hi"], at("q_hi", it, c, 1))
                    low(q_rep[64:128], ring_t[64:128, 1, :].rearrange("p (g t) -> p g t", t=T), 1.0, q_rep[64:128]).then_inc(sems["q_lo"], 1)
                if exists(it, j):
                    context_chunk(it, j, "cv", 0)
                if exists(it, p):
                    dve.wait_ge(sems["ot_hi"], at("ot_hi", it, p, 1))
                    low(o_tg[:, LO, :], ring_t[:, 0, 0:T], 1.0, o_tg[:, HI, :]).then_inc(sems["ot_lo"], 1)
                if exists(it, j):
                    context_chunk(it, j, "cv", 1)

            for j in range(-2, SLOTS):
                slot(0, j)
            with dve.Fori(1, NIT - 1) as it:
                for j in range(SLOTS):
                    slot(it, j)
            for j in range(SLOTS):
                slot(NIT - 1, j)
            for j in range(TAIL):
                slot(NIT, j)

        @block.tensor
        def _(pe):
            def split_product(out, terms):
                passes = [(a[x], b[y]) for a, b in terms for x, y in ((HI, HI), (HI, LO), (LO, HI))]
                for n, (a, b) in enumerate(passes):
                    ins = pe.matmul(out, a, b, start=(n == 0), stop=(n == len(passes) - 1))
                return ins

            def hl(f):
                return f(HI), f(LO)

            pe.wait_ge(ident_ready, 1)
            for n in range(2):
                pe.wait_ge(load_qk, 32 * (n + 1))
                k = n * PREP
                blocks = [(st_wq[:, c * P:(c + 1) * P]) for c in range(NOC)]
                blocks += [(st_wk[:, kc, c * P:(c + 1) * P]) for c in range(NOC) for kc in range(KC)]
                for q in range(0, len(blocks), 4):
                    if k >= NB:
                        pe.wait_ge(prep_free, k - NB + 1)
                    for m in range(4):
                        ins = pe.transpose(prep_banks[k % NB][:, m * P:(m + 1) * P], blocks[q + m], ident[:, :])
                    ins.then_inc(prep_raw, 1)
                    k += 1
                pe.wait_ge(prep_free, n * PREP + NTQ + NTK)
                for q in range(0, H * KC, 4):
                    if k >= NB:
                        pe.wait_ge(prep_free, k - NB + 1)
                    for m in range(4):
                        place, kc = divmod(q + m, KC)
                        r, pair = place // NOC * MD, place % NOC
                        ins = pe.matmul(prep_banks[k % NB][:, m * P:(m + 1) * P], wk_t[r:r + MD, pair, kc * P:(kc + 1) * P],
                                        wq_t[r:r + MD, pair, :], start=True, stop=True)
                    ins.then_inc(prep_raw, 1)
                    k += 1
            pe.wait_ge(prep_free, 2 * PREP)
            pe.wait_ge(vo_free, 4)
            pe.wait_ge(consts_pool, CONSTS)
            pe.wait_ge(dve_ready, 1 + 2 * (KVG + KC * KVG + 2))
            pe.wait_ge(dve_step, DVE_STEPS)

            def turn_context(it, j):
                st = stream(j)
                pe.wait_ge(load_c[st], 16 * (round_of(it, j) + 1))
                for kc in range(KC):
                    ins = pe.transpose(ring_t[:, 1, kc * S:(kc + 1) * S], ctx_nat[st][:, kc * P:(kc + 1) * P], ident[0:S, 0:S])
                ins.then_inc(sems["ct_raw"], 1)

            def turn_x(it, j):
                st = stream(j)
                pe.wait_ge(load_x[st], 16 * (round_of(it, j) + 1))
                pe.transpose(ring_t[:, 0, X_IN], x_nat[st][:, :], ident[:, :]).then_inc(sems["x_in"], 1)

            def context_chunk(it, j, fam, k):
                st, n = stream(j), layer(j) // 2
                b = bank_of(j, fam, k)
                if layer(j) == 0:
                    pe.wait_ge(sems["ct_lo"], at("ct_lo", it, j, 1))
                if last := bank_before(it, j, fam, k):
                    item, prev, i = last
                    pe.wait_ge(sems[prev + "_lo"], at(prev + "_lo", it, item, i + 1))
                ct = ctx_t[st]
                if is_gqa(j):
                    for g in range(KVG):
                        split_product(ring_c[:, b, g * S:(g + 1) * S],
                                      [(hl(lambda i: wk_r[n][:, i, kc, g].rearrange("p a d -> p (a d)")), hl(lambda i: ct[:, i, kc, :]))
                                       for kc in range(KC)])
                    ins = split_product(ring_c[0:S, b, V_COL:V_COL + KVG * GD],
                                        [(hl(lambda i: ct[:, i, kc, :]), hl(lambda i: wv_g[n][:, i, kc, :])) for kc in range(KC)])
                elif fam == "ctx":
                    h0, h1 = G_CHUNKS[k]
                    for h in range(h0, h1):
                        ins = split_product(ring_c[:, b, (h - h0) * S:(h - h0 + 1) * S],
                                            [(hl(lambda i: m_w[n][:, i, m_place(h), kc, :]), hl(lambda i: ct[:, i, kc, :])) for kc in range(KC)])
                else:
                    n0, n1 = V_CHUNKS[k]
                    ins = split_product(ring_c[0:S, b, :],
                                        [(hl(lambda i: ct[:, i, kc, :]), hl(lambda i: wv_m[n][:, i, kc, n0:n1])) for kc in range(KC)])
                ins.then_inc(sems[fam + "_raw"], 1)

            def values(it, j, k):
                if k == 0:
                    if not is_gqa(j):
                        pe.wait_ge(sems["cv_lo"], at("cv_lo", it, j, len(V_CHUNKS)))
                    else:
                        pe.wait_ge(sems["ctx_lo"], at("ctx_lo", it, j, 1))
                for part in ("hi", "lo"):
                    pe.wait_ge(sems[f"turned_{part}{k}"], at(f"turned_{part}{k}", it, j, 16))
                for h in range(k * HALF, (k + 1) * HALF):
                    if is_gqa(j):
                        v, o = v_gqa[j // 2 % 2][:, h // R], h * 2 * (GD + 1)
                        pe.matmul(so_flat[:, o:o + 2 * (GD + 1)], p_t[j % 2][:, HI, h, :], v[:, :, :].rearrange("p a d -> p (a d)"), start=True, stop=False)
                        ins = pe.matmul(so_flat[:, o:o + GD + 1], p_t[j % 2][:, LO, h, :], v[:, HI, :], start=False, stop=True)
                    else:
                        o = (h % HEADS_O) * (MD + 1)
                        out, v = so[:, h // HEADS_O, o:o + MD + 1], hl(lambda i: v_mha[j // 2 % 2][:, i, h, :])
                        ins = split_product(out, [(hl(lambda i: p_t[j % 2][:, i, h, :]), v)])
                    if h == H - 1 or (h == 2 * HEADS_O - 1 and not is_gqa(j)):
                        ins.then_inc(sems["o_raw"], 1)

            def turn_o(it, j):
                pe.wait_ge(sems["o_norm"], at("o_norm", it, j, 1))
                pe.transpose(ring_t[:, 0, 0:T], o_ng[:, :], ident[:, :]).then_inc(sems["ot_raw"], 1)

            def output(it, j):
                n = layer(j) // 2
                if is_gqa(j):
                    pe.wait_ge(sems["ot_lo"], at("ot_lo", it, j, 1))
                    split_product(ring_t[:, 0, Y_GQA], [(hl(lambda i: wo_g[n][:, i, :]), hl(lambda i: o_tg[:, i, :]))]).then_inc(sems["yg_raw"], 1)
                    return
                if exists(it, j - 2):
                    name, item = ("out", j - 2) if layer(j - 2) == LAYERS - 1 else ("xg_f32", following(j - 2))
                    pe.wait_ge(sems[name], at(name, it, item, 1))
                for part in ("hi", "lo"):
                    pe.wait_ge(sems["turned_o_" + part], at("turned_o_" + part, it, j, 16))
                terms = [(hl(lambda i: wo_m[n][:, i, c, :]), hl(lambda i: o_t[:, i, c, :])) for c in range(NOC)]
                if layer(j) == LAYERS - 1:
                    terms = [(b, a) for a, b in terms]
                split_product(misc[:, 0:P], terms).then_inc(sems["ym_raw"], 1)

            def scores(it, j):
                st, n = stream(j), layer(j) // 2
                if exists(it, j - 2):
                    pe.wait_ge(sems["o_norm"], at("o_norm", it, j - 2, n_o[layer(j - 2)]))
                if is_gqa(j):
                    pe.wait_ge(sems["sq"], at("sq", it, j, 1))
                    pe.matmul(so_flat[:, SS_COL:SS_COL + 1], x_sq[st][:, :], ones[:, :], start=True, stop=True)
                    pe.wait_ge(sems["kb"], at("kb", it, j, 1))
                    pe.wait_ge(sems["q_lo"], at("q_lo", it, j, 1))
                    kb = k_bd[:, :, :, :].rearrange("p g r s -> p (g r s)")
                    for g in range(KVG):
                        a = g * R * S
                        while a < (g + 1) * R * S:
                            e = min((g + 1) * R * S, (a // BANK + 1) * BANK)
                            ins = pe.matmul(so_flat[:, a:e], q_rep[:, g, :], kb[:, a:e], start=True, stop=True)
                            a = e
                    ins.then_inc(sems["s_raw"], 1)
                else:
                    pe.wait_ge(sems["xm_lo"], at("xm_lo", it, j, 1))
                    pe.wait_ge(sems["ctx_lo"], at("ctx_lo", it, j, len(G_CHUNKS)))
                    ind = bias_r[n][:, :, :].rearrange("p h s -> p (h s)")
                    for a in range(0, HS, BANK):
                        e = min(HS, a + BANK)
                        pe.matmul(so_flat[:, a:e], bias_l[:, :], ind[:, a:e], start=True, stop=False)
                        for x, y in ((HI, HI), (HI, LO), (LO, HI)):
                            ins = pe.matmul(so_flat[:, a:e], x_s[st][:, x, :], g_s[:, y, a:e], start=False, stop=(x == LO))
                        ins.then_inc(sems["s_raw"], 1)

            def queries(it, j):
                st, n = stream(j), layer(j) // 2
                pe.wait_ge(sems["xg_lo"], at("xg_lo", it, j, 1))
                for g in range(KVG):
                    ins = split_product(ring_t[:, 1, g * T:(g + 1) * T],
                                        [(hl(lambda i: wq_r[n][:, i, g].rearrange("p a d -> p (a d)")), hl(lambda i: x_s[st][:, i, :]))])
                ins.then_inc(sems["q_raw"], 1)

            def slot(it, j):
                c, p, o, e, u = j + 1, j - 1, j - 2, j + 2, j - 3
                mine = [a for a in chunks(j) if exists(it, a[0])]
                if exists(it, j):
                    scores(it, j)
                if is_gqa(j):
                    if exists(it, o):
                        pe.wait_ge(sems["ot_lo"], at("ot_lo", it, o, 1))
                    if exists(it, u) and layer(u) == LAYERS - 1:
                        pe.wait_ge(sems["xb"], at("xb", it, u, 1))
                        if exists(it, u - 2) and layer(u - 2) == LAYERS - 1:
                            pe.wait_ge(sems["xr"], at("xr", it, u - 2, 1))
                        pe.transpose(ring_t[:, 1, X_RES], x_b[stream(u)][:, :], ident[:, :]).then_inc(sems["xr_raw"], 1)
                    if layer(e) == 0 and exists(it, e):
                        turn_x(it, e)
                        turn_context(it, e)
                    for a in mine[:1]:
                        context_chunk(it, *a)
                    if exists(it, o):
                        output(it, o)
                    for a in mine[1:2]:
                        context_chunk(it, *a)
                else:
                    if exists(it, c):
                        context_chunk(it, c, "ctx", 0)
                    if exists(it, j):
                        context_chunk(it, j, "cv", 0)
                if exists(it, p):
                    if exists(it, j):
                        pe.wait_ge(sems["s_sub"], at("s_sub", it, j, 2))
                    values(it, p, 0)
                    values(it, p, 1)
                if is_gqa(j):
                    for a in mine[2:]:
                        context_chunk(it, *a)
                    if exists(it, u):
                        output(it, u)
                    return
                if exists(it, c):
                    if exists(it, j - 4) and layer(j - 4) == LAYERS - 1:
                        pe.wait_ge(sems["xr"], at("xr", it, j - 4, 1))
                    queries(it, c)
                if exists(it, j):
                    context_chunk(it, j, "cv", 1)
                if exists(it, p):
                    turn_o(it, p)

            for j in range(-2, SLOTS):
                slot(0, j)
            with pe.Fori(1, NIT - 1) as it:
                for j in range(SLOTS):
                    slot(it, j)
            for j in range(SLOTS):
                slot(NIT - 1, j)
            for j in range(TAIL):
                slot(NIT, j)


CONSTS = 15
ARENA = 11484
SMALL_LOADS = 20
DVE_STEPS = 52


_GQA = ("wq", "wk", "wv", "wo", "norm_w")
_MHA = {"Wq": "Wq", "Wk": "Wk", "Wv": "Wv", "Wo": "Wo", "bo": "bo",
        "tok_a": "token_indices_A", "tok_b": "token_indices_B"}


def kernel(**inputs):
    import numpy as _np
    import concourse.bacc as _bacc
    from concourse import mybir as _mybir
    from concourse.bass_utils import run_bass_kernel_spmd as _run

    nc = _bacc.Bacc("TRN2", target_bir_lowering=False, num_devices=1)
    arrays = {}

    def given(name):
        a = _np.ascontiguousarray(inputs[name])
        arrays[f"in_{name}_dram"] = a
        return nc.dram_tensor(f"in_{name}_dram", a.shape, _mybir.dt.from_np(a.dtype), kind="ExternalInput").ap()

    x, ctx = given("x"), given("ctx_2048")
    mask_a, mask_b = given("mask_S_fk1"), given("mask_S_fk0")
    gqa = [{k: given(f"L{n}_xattn_{k}") for k in _GQA} for n in (0, 2)]
    mha = [{k: given(f"L{n}_xattn_{v}") for k, v in _MHA.items()} for n in (1, 3)]
    out = nc.dram_tensor("out_0_dram", x.shape, _mybir.dt.float32, kind="ExternalOutput").ap()
    build(nc, x, ctx, mask_a, mask_b, gqa, mha, out)
    r = _run(nc, [arrays], core_ids=[0])
    return r.results[0]["out_0_dram"]
```
